# Optimizing a Trainium2 kernel written in Bass

```python
import numpy as np
import jax
import jax.numpy as jnp

def _softmax(x, axis=-1):
    return jax.nn.softmax(x, axis=axis)

def _gelu(x):
    return jax.nn.gelu(x, approximate=True)

def _silu(x):
    return jax.nn.silu(x)

def _sigmoid(x):
    return jax.nn.sigmoid(x)

def _layernorm(x, axis=-1, eps=1e-05):
    m = jnp.mean(x, axis=axis, keepdims=True)
    v = jnp.var(x, axis=axis, keepdims=True)
    return (x - m) / jnp.sqrt(v + eps)

def _scatter_add(tgt, idx, src, axis=0):
    return tgt.at[idx].add(src)

def _segment_sum(src, seg, n):
    return jax.ops.segment_sum(src, seg, n)
kernel_name = 'mk_decoder_preln_d1_seqx_r8_2ab441'

def setup_inputs(seed: int=0):
    np.random.seed(seed)
    _w = jnp.asarray

    def _rec_inputs():
        import jax
        import jax.numpy as jnp
        _rk = jax.random.key(seed)
        x = 7.22e-05 + 1 * jax.random.normal(jax.random.fold_in(_rk, 1), (4, 256, 128), jnp.float32)
        _lenS = 256 - jax.random.randint(jax.random.fold_in(_rk, 7), (4,), 0, max(1, 256 // 4) + 1, jnp.int32)
        _lenS2 = 256 - jax.random.randint(jax.random.fold_in(_rk, 8), (4,), 0, max(1, 256 // 4) + 1, jnp.int32)
        _ctx_1024P = jax.random.normal(jax.random.fold_in(_rk, 11), (4, 16, 128), jnp.float32)
        _ctx_1024c = jax.random.dirichlet(jax.random.fold_in(_rk, 511), 0.3 * jnp.ones((16,), jnp.float32), (4, 256))
        _ctx_1024t = jnp.einsum('bsk,bkd->bsd', _ctx_1024c, _ctx_1024P)
        _ctx_1024t = _ctx_1024t * jax.lax.rsqrt(jnp.mean(jnp.square(_ctx_1024t)) + 1e-12) * 0.953939
        ctx_1024 = 4.13588e-05 + 0.999923 * (_ctx_1024t + 0.3 * jax.random.normal(jax.random.fold_in(_rk, 611), (4, 256, 128), jnp.float32))
        return (x, ctx_1024)
    x, ctx_1024 = _rec_inputs()

    def _L0_attn_setup():
        import jax, jax.numpy as jnp
        import numpy as np
        D_MODEL = 128
        N_HEADS = 16
        D_HEAD = 64
        B, S = (8, 128)
        EPS = 1.1920929e-07
        key = jax.random.key(seed)
        k1, k2, k3 = jax.random.split(key, 3)
        x = jax.random.normal(k1, (B, S, D_MODEL), dtype=jnp.float32)
        W_qkv = jax.random.normal(k2, (3 * N_HEADS * D_HEAD, D_MODEL), dtype=jnp.float32) * 0.02
        b_qkv = jnp.zeros((3 * N_HEADS * D_HEAD,), dtype=jnp.float32)
        W_o = jax.random.normal(k3, (D_MODEL, N_HEADS * D_HEAD), dtype=jnp.float32) * 0.02
        b_o = jnp.zeros((D_MODEL,), dtype=jnp.float32)
        return {'x': x, 'W_qkv': W_qkv, 'b_qkv': b_qkv, 'W_o': W_o, 'b_o': b_o}
    _L0_attn_all = _L0_attn_setup()
    _L0_attn_in = {k: v for k, v in _L0_attn_all.items() if k in ('W_qkv', 'b_qkv', 'W_o', 'b_o')}
    del _L0_attn_all

    def _L0_xattn_setup():
        import jax, jax.numpy as jnp
        import numpy as np
        D_MODEL = 128
        NUM_HEADS = 16
        D_K = D_MODEL // NUM_HEADS
        B, S = (4, 256)
        key = jax.random.key(seed)
        ks = jax.random.split(key, 11)
        scale = 1.0 / np.sqrt(D_MODEL)
        inp = {'query': jax.random.normal(ks[0], (B, S, D_MODEL), dtype=jnp.float32), 'key': jax.random.normal(ks[1], (B, S, D_MODEL), dtype=jnp.float32), 'value': jax.random.normal(ks[2], (B, S, D_MODEL), dtype=jnp.float32), 'Wq': jax.random.normal(ks[3], (D_MODEL, D_MODEL), dtype=jnp.float32) * scale, 'bq': jnp.zeros((D_MODEL,), dtype=jnp.float32), 'Wk': jax.random.normal(ks[4], (D_MODEL, D_MODEL), dtype=jnp.float32) * scale, 'bk': jnp.zeros((D_MODEL,), dtype=jnp.float32), 'Wv': jax.random.normal(ks[5], (D_MODEL, D_MODEL), dtype=jnp.float32) * scale, 'bv': jnp.zeros((D_MODEL,), dtype=jnp.float32), 'Wo': jax.random.normal(ks[6], (D_MODEL, D_MODEL), dtype=jnp.float32) * scale, 'bo': jnp.zeros((D_MODEL,), dtype=jnp.float32)}
        return inp
    _L0_xattn_all = _L0_xattn_setup()
    _L0_xattn_in = {k: v for k, v in _L0_xattn_all.items() if k in ('Wq', 'bq', 'Wk', 'bk', 'Wv', 'bv', 'Wo', 'bo')}
    del _L0_xattn_all

    def _L0_ffn_setup():
        import jax, jax.numpy as jnp
        import numpy as np
        K = 2
        key = jax.random.key(seed)
        ks = jax.random.split(key, 7)
        B, S, D, E = (2, 256, 128, 8)
        H = 4 * D
        sd = 1.0 / np.sqrt(D)
        sh = 1.0 / np.sqrt(H)
        return {'x': jax.random.normal(ks[0], (B, S, D), jnp.float32), 'Wr': jax.random.normal(ks[1], (D, E), jnp.float32) * sd, 'br': jax.random.normal(ks[2], (E,), jnp.float32) * sd, 'W1': jax.random.normal(ks[3], (E, D, H), jnp.float32) * sd, 'b1': jax.random.normal(ks[4], (E, H), jnp.float32) * sd, 'W2': jax.random.normal(ks[5], (E, H, D), jnp.float32) * sh, 'b2': jax.random.normal(ks[6], (E, D), jnp.float32) * sh}
    _L0_ffn_all = _L0_ffn_setup()
    _L0_ffn_in = {k: v for k, v in _L0_ffn_all.items() if k in ('Wr', 'br', 'W1', 'b1', 'W2', 'b2')}
    del _L0_ffn_all
    return {'x': x, 'ctx_1024': ctx_1024, 'L0_attn_W_qkv': _L0_attn_in['W_qkv'], 'L0_attn_b_qkv': _L0_attn_in['b_qkv'], 'L0_attn_W_o': _L0_attn_in['W_o'], 'L0_attn_b_o': _L0_attn_in['b_o'], 'L0_xattn_Wq': _L0_xattn_in['Wq'], 'L0_xattn_bq': _L0_xattn_in['bq'], 'L0_xattn_Wk': _L0_xattn_in['Wk'], 'L0_xattn_bk': _L0_xattn_in['bk'], 'L0_xattn_Wv': _L0_xattn_in['Wv'], 'L0_xattn_bv': _L0_xattn_in['bv'], 'L0_xattn_Wo': _L0_xattn_in['Wo'], 'L0_xattn_bo': _L0_xattn_in['bo'], 'L0_ffn_Wr': _L0_ffn_in['Wr'], 'L0_ffn_br': _L0_ffn_in['br'], 'L0_ffn_W1': _L0_ffn_in['W1'], 'L0_ffn_b1': _L0_ffn_in['b1'], 'L0_ffn_W2': _L0_ffn_in['W2'], 'L0_ffn_b2': _L0_ffn_in['b2']}

def reference(x, ctx_1024, L0_attn_W_qkv, L0_attn_b_qkv, L0_attn_W_o, L0_attn_b_o, L0_xattn_Wq, L0_xattn_bq, L0_xattn_Wk, L0_xattn_bk, L0_xattn_Wv, L0_xattn_bv, L0_xattn_Wo, L0_xattn_bo, L0_ffn_Wr, L0_ffn_br, L0_ffn_W1, L0_ffn_b1, L0_ffn_W2, L0_ffn_b2):
    import jax
    import jax.numpy as jnp

    def _L0_attn_ref(x, W_qkv, b_qkv, W_o, b_o):
        import jax, jax.numpy as jnp
        import numpy as np
        D_MODEL = 128
        N_HEADS = 16
        D_HEAD = 64
        B, S = (8, 128)
        EPS = 1.1920929e-07
        normed = x * jax.lax.rsqrt(jnp.mean(x * x, axis=-1, keepdims=True) + EPS)
        qkv = normed @ W_qkv.T + b_qkv
        qkv = qkv.reshape(*qkv.shape[:-1], N_HEADS, D_HEAD, 3)
        q, k, v = (qkv[..., 0], qkv[..., 1], qkv[..., 2])
        scores = jnp.einsum('bqhd,bkhd->bhqk', q, k)
        seq = x.shape[-2]
        causal_mask = jnp.triu(jnp.ones((seq, seq), dtype=bool), k=1)
        scores = jnp.where(causal_mask, -jnp.inf, scores)
        attn = jax.nn.softmax(scores, axis=-2)
        z = jnp.einsum('bhqk,bkhd->bqhd', attn, v)
        z = z.reshape(*z.shape[:-2], N_HEADS * D_HEAD)
        return z @ W_o.T + b_o

    def _L0_xattn_ref(query, key, value, Wq, bq, Wk, bk, Wv, bv, Wo, bo):
        import jax, jax.numpy as jnp
        import numpy as np
        D_MODEL = 128
        NUM_HEADS = 16
        D_K = D_MODEL // NUM_HEADS
        B, S = (4, 256)
        b, sq, _ = query.shape
        sk = key.shape[1]
        Q = query @ Wq + bq
        K = key @ Wk + bk
        V = value @ Wv + bv
        Q = Q.reshape(b, sq, NUM_HEADS, D_K).transpose(0, 2, 1, 3)
        K = K.reshape(b, sk, NUM_HEADS, D_K).transpose(0, 2, 1, 3)
        V = V.reshape(b, sk, NUM_HEADS, D_K).transpose(0, 2, 1, 3)
        scores = jnp.einsum('bhqd,bhkd->bhqk', Q, K) / jnp.sqrt(jnp.float32(D_K))
        attn = jax.nn.softmax(scores, axis=-1)
        out = jnp.einsum('bhqk,bhkd->bhqd', attn, V)
        out = out.transpose(0, 2, 1, 3).reshape(b, sq, D_MODEL)
        return out @ Wo + bo

    def _L0_ffn_ref(x, Wr, br, W1, b1, W2, b2):
        import jax, jax.numpy as jnp
        import numpy as np
        K = 2
        E = Wr.shape[-1]
        scores = jnp.einsum('bsd,de->bse', x, Wr) + br
        _, topk_idx = jax.lax.top_k(scores, K)
        indicator = jax.nn.one_hot(topk_idx, E, dtype=scores.dtype).sum(-2)
        neg_inf = jnp.asarray(-jnp.inf, scores.dtype)
        weights = jax.nn.softmax(jnp.where(indicator > 0, scores, neg_inf), axis=-1)
        out = jnp.zeros_like(x)
        for i in range(E):
            xi = x * indicator[..., i:i + 1]
            h = jax.nn.relu(jnp.einsum('bsd,dh->bsh', xi, W1[i]) + b1[i])
            yi = jnp.einsum('bsh,hd->bsd', h, W2[i]) + b2[i]
            out = out + yi * weights[..., i:i + 1]
        return out
    x = x + _L0_attn_ref(_layernorm(x, axis=-1), L0_attn_W_qkv, L0_attn_b_qkv, L0_attn_W_o, L0_attn_b_o)
    x = x + _L0_xattn_ref(_layernorm(x, axis=-1), ctx_1024, ctx_1024, L0_xattn_Wq, L0_xattn_bq, L0_xattn_Wk, L0_xattn_bk, L0_xattn_Wv, L0_xattn_bv, L0_xattn_Wo, L0_xattn_bo)
    x = x + _L0_ffn_ref(_layernorm(x, axis=-1), L0_ffn_Wr, L0_ffn_br, L0_ffn_W1, L0_ffn_b1, L0_ffn_W2, L0_ffn_b2)
    return x

_drawn_inputs = setup_inputs


def setup_inputs(seed=0):
    import zlib

    import numpy as np

    out = dict(_drawn_inputs(seed))
    spreads = {'L0_attn_b_qkv': (0.0, 0.1),
     'L0_attn_b_o': (0.0, 0.1),
     'L0_xattn_bq': (0.0, 0.1),
     'L0_xattn_bk': (0.0, 0.1),
     'L0_xattn_bv': (0.0, 0.1),
     'L0_xattn_bo': (0.0, 0.1)}
    factors = {}
    for name, (base, spread) in spreads.items():
        noise = np.random.default_rng([zlib.crc32(name.encode()), seed]).standard_normal(out[name].shape)
        drawn = base * np.exp(spread * noise) if base else spread * noise
        out[name] = jnp.asarray(drawn.astype(out[name].dtype))
    for name, factor in factors.items():
        out[name] = (out[name] * factor).astype(out[name].dtype)
    return out
```

```python
from contextlib import ExitStack

import concourse.bass as bass
from concourse import mybir

F32 = mybir.dt.float32
BF16 = mybir.dt.bfloat16
U32 = mybir.dt.uint32
ALU = mybir.AluOpType
ACT = mybir.ActivationFunctionType
AX = mybir.AxisListType.X

P = 128
B, S, D = 4, 256, 128
NT = B * S // P
TPB = S // P
H, E1 = 16, 64
HP = H // 2
DH = 8
NE, HID = 8, 512
NC = HID // P
EPS_LN, EPS_RMS = 1e-5, 1.1920929e-07
MASKED = -1.0e38
PARTS_Q = (0, 0, 0, 1, 1, 2)
PARTS_K = (0, 1, 2, 0, 1, 0)
MAX_ROW = DH * len(PARTS_Q)
SCALE_X = float(DH) ** -0.5


def ge(eng, sem, value):
    if value > 0:
        eng.wait_ge(sem, value)


def decoder_layer(nc, x, ctx_in, w_qkv, b_qkv, w_o, b_o, wq, bq, wk, bk, wv, bv, wo, bo,
                  wr, br, w1, b1, w2, b2, out):
    ctx = ExitStack()
    with ctx:
        def sb(name, shape, dt=F32):
            return ctx.enter_context(nc.sbuf_tensor(name, shape, dt))

        def sem(name):
            return ctx.enter_context(nc.semaphore(name))

        resid = sb("resid", [P, NT, D])
        w_in = sb("w_in", [P, 4096])
        w_nat = w_in[:, 0:3072].rearrange("p (hh c d) -> p hh c d", c=3, d=D)
        wv_c = w_in[:, 3072:4096].rearrange("p (hh d) -> p hh d", d=D)
        w1_sb = w_in[:, :].rearrange("p (e n) -> p e n", n=HID)
        wk_g = sb("wk_g", [P, 4096])
        wk_blk = wk_g[:, 0:2048].rearrange("p (hh n) -> p hh n", n=2 * D)
        G = wk_g[:, 2048:4096].rearrange("p (h n) -> p h n", n=D)
        q_st = wk_g[:, :].bitcast(BF16).rearrange("p (r g n) -> p r g n", r=2, g=HP)
        b_nat = sb("b_nat", [P, HP, 3])
        row_add = sb("row_add", [P, 2, HP])
        cvec = sb("cvec", [P, H])
        wvT = sb("wvT", [P, H * E1])
        woT = sb("woT", [P, HP, D])
        normT = sb("normT", [P, NT * P])
        nk = sb("nk", [P, 2, S])
        t_p = sb("t_p", [P, 2 * H * S])
        t_sb = t_p[:, :].rearrange("p (r h q) -> p r h q", r=2, h=H)
        px = t_p[:, 0:4096].rearrange("p (r n) -> p r n", r=2)
        hid = t_p[:, 4096:8192].rearrange("p (r c n) -> p r c n", r=2, c=NC)
        p01 = sb("p01", [P, H * S + H * P])
        p0 = p01[:, 0:H * S].rearrange("p (h q) -> p h q", h=H)
        p1 = p01[:, H * S:].rearrange("p (h q) -> p h q", h=H)
        w2_sb = p01[:, 0:4096].rearrange("p (n d) -> p n d", d=D)
        negmax = sb("negmax", [P, 2, H])
        psums = sb("psums", [P, 2, H])
        rsum = sb("rsum", [P, 2, H])
        v_sb = sb("v_sb", [P, 2, H * E1])
        zT = sb("zT", [P, HP, S])
        norm = sb("norm", [P, NT, D])
        stats = sb("stats", [P, NT, 6])
        mv = sb("mv", [P, 3, NT, 2])
        rstd = sb("rstd", [P, 3, NT])
        tmp8 = sb("tmp8", [P, 3, NT])
        negm = sb("negm", [P, 3, NT])
        ctx_nat = zT[:, :, 0:D]
        ctxT = v_sb[:, 0, :]
        k_f = v_sb[:, 1, :]
        k_r = p01[:, 0:1024]
        wo_nat = p01[:, 1024:2048]
        k_part = sb("k_part", [P, 3, NT * P], BF16)
        k_max = sb("k_max", [P, HP, NT * P], BF16)
        k_exp = sb("k_exp", [P, HP, NT * P], BF16)
        v_pad = sb("v_pad", [P, NT, H, 32])
        n2T = sb("n2T", [P, S])
        q_f = sb("q_f", [P, S])
        q_r = sb("q_r", [P, S])
        q_part = sb("q_part", [P, 3, S], BF16)
        mneg = sb("mneg", [P, TPB, H])
        m_f = sb("m_f", [H, S])
        m_r = sb("m_r", [H, S])
        m_part = sb("m_part", [H, 3, S], BF16)
        o_raw = sb("o_raw", [P, 4, S])
        r_den = sb("r_den", [P, TPB, 16])
        o_n = sb("o_n", [P, TPB, D])
        oT = sb("oT", [P, S])
        wx = sb("wx", [P, 4, D])
        wqk = sb("wqk", [P, 2, D])
        bqk = sb("bqk", [P, 2])
        brow = sb("brow", [P, 4, D])
        wr_sb = sb("wr_sb", [P, NE])
        br_row = sb("br_row", [P, NE])
        b1_nat = sb("b1_nat", [NE * NC, P])
        b1T = sb("b1T", [P, NE * NC])
        b2_sb = sb("b2_sb", [NE, D])
        ident = sb("ident", [P, P])
        ident_b = sb("ident_b", [P, P], BF16)
        mask = sb("mask", [P, 4, P], BF16)
        half = sb("half", [P, NT])
        score = sb("score", [P, NT, NE])
        top = sb("top", [P, NT, 8])
        top_i = sb("top_i", [P, NT, 8], U32)
        top_f = sb("top_f", [P, NT, 2])
        iota8 = sb("iota8", [P, NE])
        gate = sb("gate", [P, 4, NT])
        hot = sb("hot", [P, 2, NT, NE])
        wgt = sb("wgt", [P, NT, NE])
        wgtT = wvT[0:NE, :]


        ps = ctx.enter_context(nc.psum_tensor("ps", [P, 8, 512], F32))

        s_x, s_bias, s_wo, s_ctx, s_wx, s_ffnb = (sem(n) for n in ("s_x", "s_bias", "s_wo", "s_ctx", "s_wx", "s_ffnb"))
        s_w = [sem(f"s_wqkv{i}") for i in range(4)]
        s_w1, s_w2, s_out = sem("s_w1"), sem("s_w2"), sem("s_out")
        s_const = sem("s_const")
        s_pool = sem("s_pool")
        s_dve = sem("s_dve")
        s_bn, s_mv, s_rstd, s_n1 = sem("s_bn"), sem("s_mv"), sem("s_rstd"), sem("s_n1")
        s_wprep = sem("s_wprep")
        s_set, s_set_ev = sem("s_set"), sem("s_set_ev")
        s_vx, s_vx_ev = sem("s_vx"), sem("s_vx_ev")
        s_nk = sem("s_nk")
        s_xb = sem("s_xb")
        s_kpart, s_kst = sem("s_kpart"), sem("s_kst")
        s_sc, s_max, s_exp = sem("s_sc"), sem("s_max"), sem("s_exp")
        s_tv, s_tv_ev = sem("s_tv"), sem("s_tv_ev")
        s_z, s_z_ev, s_wo1, s_x1 = sem("s_z"), sem("s_z_ev"), sem("s_wo1"), sem("s_x1")
        s_mv2, s_n2, s_xb2 = sem("s_mv2"), sem("s_n2"), sem("s_xb2")
        s_misc, s_misc_ev = sem("s_misc"), sem("s_misc_ev")
        s_qpart, s_qfree = sem("s_qpart"), sem("s_qfree")
        s_qst = [sem("s_qst0"), sem("s_qst1")]
        s_mst = [sem("s_mst0"), sem("s_mst1")]
        s_mx, s_mx_ev, s_mpart = sem("s_mx"), sem("s_mx_ev"), sem("s_mpart")
        s_st, s_px, s_pv, s_pv_ev = sem("s_st"), sem("s_px"), sem("s_pv"), sem("s_pv_ev")
        s_mv3, s_n3 = sem("s_mv3"), sem("s_n3")
        s_n3T, s_rt, s_score, s_ed, s_wgt, s_wT, s_wTe = (sem(n) for n in ("s_n3T", "s_rt", "s_score", "s_ed", "s_wgt", "s_wT", "s_wTe"))
        s_b2, s_acc0 = sem("s_b2"), sem("s_acc0")
        s_h, s_ha, s_hd, s_y, s_acc = sem("s_h"), sem("s_ha"), sem("s_hd"), sem("s_y"), sem("s_acc")

        tiles = "b (i p) d -> p (b i) d"

        def t_unit(b, u):
            return u if b == 0 else HP + 12 * (b - 1) + u

        def v_unit(b, u):
            return HP + 12 * b + (HP if b < B - 1 else 0) + u

        misc_order = []
        misc_order += [("n2T", 0), ("q", 0), ("n2T", 1), ("q", 1), ("mT", 0)]
        for b in range(B):
            if b >= 1:
                misc_order += [("oq0", b - 1), ("oT0", b - 1), ("oq1", b - 1), ("oT1", b - 1), ("wo", b - 1)]
            if b + 2 < B:
                misc_order += [("n2T", b + 2), ("q", b + 2)]
            if b + 1 < B:
                misc_order += [("mT", b + 1)]
        misc_order += [(k, B - 1) for k in ("oq0", "oT0", "oq1", "oT1", "wo")]
        misc_at = {k: i for i, k in enumerate(misc_order)}

        block = ctx.enter_context(nc.Block())

        @block.sync
        def _(sp):
            sp.dma_start(resid[:, :, :], x.rearrange(tiles, p=P)).then_inc(s_x, 16)
            w_view = w_qkv.rearrange("(hh p c) d -> p hh (c d)", p=P, c=3)
            sp.dma_start(b_nat[:, :, :], b_qkv.rearrange("(hh p c) -> p hh c", p=P, c=3)).then_inc(s_bias, 16)
            for i in range(4):
                sp.dma_start(w_in[:, 768 * i:768 * (i + 1)].rearrange("p (hh n) -> p hh n", hh=2),
                             w_view[:, 2 * i:2 * i + 2, :]).then_inc(s_w[i], 16)
            sp.wait_ge(s_kpart, 3)
            sp.wait_ge(s_const, 6)
            for k_stack in (k_max, k_exp):
                for par in range(2):
                    for n, part in enumerate(PARTS_K):
                        r = 64 * par + DH * n
                        sp.dma_start(k_stack[r:r + DH, :, :],
                                     k_part[64 * par:64 * par + 64, part, :]
                                     ).then_inc(s_kst, 16)

            def stack_q(b):
                sp.wait_ge(s_qpart, 3 * (b + 1))
                ge(sp, s_st, HP * (b - 1))
                for par in range(2):
                    for n, part in enumerate(PARTS_Q):
                        r = 64 * par + DH * n
                        sp.dma_start(q_st[r:r + DH, b % 2, :, S * par:S * par + S],
                                     q_part[64 * par:64 * par + 64, part, :]
                                     ).then_inc(s_qst[b % 2], 16)

            def stack_m(b):
                sp.wait_ge(s_mpart, 3 * (b + 1))
                for par in range(2):
                    for part in range(3):
                        r = 64 * par + MAX_ROW + part
                        sp.dma_start(q_st[r:r + 1, b % 2, :, S * par:S * par + S],
                                     m_part[8 * par:8 * par + 8, part, :]).then_inc(s_mst[b % 2], 16)

            sp.wait_ge(s_qfree, 1)
            stack_q(0)
            stack_q(1)
            stack_m(0)
            sp.dma_start(w1_sb, w1.rearrange("e p n -> p e n")).then_inc(s_w1, 16)
            sp.wait_ge(s_z, 4 * B)
            sp.dma_start(w2_sb, w2.rearrange("e (c p) d -> p (e c) d", p=P)).then_inc(s_w2, 16)
            for b in range(B):
                if b + 2 < B:
                    stack_q(b + 2)
                if b + 1 < B:
                    stack_m(b + 1)
            for hf in range(2):
                sp.wait_ge(s_acc, 2 * NE - 1 + hf)
                sp.dma_start(out.rearrange(tiles, p=P)[:, 4 * hf:4 * hf + 4, :],
                             resid[:, 4 * hf:4 * hf + 4, :]).then_inc(s_out, 16)
            sp.wait_ge(s_out, 32)

        @block.gpsimd
        def _(pool):
            steps = [0]

            def step(ins):
                steps[0] += 1
                ins.then_inc(s_pool, 1)
                pool.wait_ge(s_pool, steps[0])

            step(pool.memset(ident[:, :], 0.0))
            pool.affine_select(out=ident[:, :], in_=ident[:, :], compare_op=ALU.not_equal, fill=1.0, base=0,
                               pattern=[[-1, P]], channel_multiplier=1).then_inc(s_const, 1)
            step(pool.memset(ident_b[:, :], 0.0))
            pool.affine_select(out=ident_b[:, :], in_=ident_b[:, :], compare_op=ALU.not_equal, fill=1.0, base=0,
                               pattern=[[-1, P]], channel_multiplier=1).then_inc(s_const, 1)
            pool.memset(wk_blk, 0.0).then_inc(s_const, 1)
            step(pool.memset(mask[:, :, :], 0.0))
            pool.affine_select(out=mask[:, :, :], in_=mask[:, :, :], compare_op=ALU.is_ge, fill=MASKED, base=0,
                               pattern=[[0, 4], [1, P]], channel_multiplier=-1).then_inc(s_const, 1)
            step(pool.memset(half[:, :], -0.5))

            def rsqrt_of_var(n, t0, cnt):
                step(pool.tensor_scalar(tmp8[:, n, t0:t0 + cnt], mv[:, n, t0:t0 + cnt, 1], EPS_LN, None, ALU.add))
                step(pool.tensor_tensor(rstd[:, n, t0:t0 + cnt], tmp8[:, n, t0:t0 + cnt], half[:, 0:cnt], ALU.pow))
                step(pool.tensor_scalar(negm[:, n, t0:t0 + cnt], mv[:, n, t0:t0 + cnt, 0], -1.0, None, ALU.mult))

            pool.wait_ge(s_mv, NT)
            rsqrt_of_var(0, 0, NT)
            step(pool.tensor_tensor(tmp8[:, 0, :], mv[:, 0, :, 1], rstd[:, 0, :], ALU.mult))
            step(pool.tensor_tensor(tmp8[:, 0, :], tmp8[:, 0, :], rstd[:, 0, :], ALU.mult))
            step(pool.tensor_scalar(tmp8[:, 0, :], tmp8[:, 0, :], EPS_RMS, None, ALU.add))
            step(pool.tensor_tensor(tmp8[:, 0, :], tmp8[:, 0, :], half[:, :], ALU.pow))
            pool.tensor_tensor(rstd[:, 0, :], rstd[:, 0, :], tmp8[:, 0, :], ALU.mult).then_inc(s_rstd, 1)

            pool.memset(k_max[:, :, :], 0.0).then_inc(s_const, 1)
            pool.memset(k_exp[:, :, :], 1.0).then_inc(s_const, 1)
            step(pool.memset(v_pad[:, :, :, :], 0.0))
            pool.memset(v_pad[:, :, :, DH:DH + 1], 1.0).then_inc(s_const, 1)
            pool.iota(iota8[:, :], pattern=[[1, NE]], base=0, channel_multiplier=0,
                      allow_small_or_imprecise_dtypes=True).then_inc(s_const, 1)

            def add_one(b):
                if b >= 2:
                    pool.wait_ge(s_tv, v_unit(b - 2, 3) + 1)
                pool.tensor_scalar(nk[:, b % 2, :], normT[:, S * b:S * b + S], 1.0, None, ALU.add).then_inc(s_nk, 1)

            def split(dst, src, rest, done):
                pool.tensor_copy(dst[0], src).then_inc(done, 1)
                pool.wait_ge(done, splits[done] + 1)
                step(pool.tensor_tensor(rest, src, dst[0], ALU.subtract))
                pool.tensor_copy(dst[1], rest).then_inc(done, 1)
                pool.wait_ge(done, splits[done] + 2)
                pool.tensor_tensor(dst[2], rest, dst[1], ALU.subtract).then_inc(done, 1)
                splits[done] += 3

            pool.wait_ge(s_wx, 144)
            pool.tensor_copy(wqk[:, :, :].rearrange("p i (r d g) -> p (i r) d g", r=2, d=DH),
                             wx[:, 0:2, :].rearrange("p i (r g d) -> p (i r) d g", r=2, d=DH)).then_inc(s_const, 1)
            splits = {s_kpart: 0, s_qpart: 0, s_mpart: 0}
            pool.wait_ge(s_set_ev, 2)
            add_one(0)
            add_one(1)
            pool.wait_ge(s_n1, NT)
            pool.wait_ge(s_wx, 144)
            pool.tensor_tensor(resid[:, :, :], resid[:, :, :],
                               brow[:, 0:1, :].to_broadcast([P, NT, D]), ALU.add).then_inc(s_xb, 1)
            pool.wait_ge(s_set_ev, 15)
            split([k_part[:, i, :] for i in range(3)], k_f, k_r, s_kpart)

            def norm_batch(n, b, s_in, s_norm):
                pool.wait_ge(s_in, TPB * (b + 1))
                rsqrt_of_var(n, TPB * b, TPB)
                for t in range(TPB * b, TPB * b + TPB):
                    pool.tensor_scalar(norm[:, t, :], resid[:, t, :], negm[:, n, t:t + 1], rstd[:, n, t:t + 1],
                                       ALU.add, ALU.mult).then_inc(s_norm, 1)

            for b in range(B):
                norm_batch(1, b, s_mv2, s_n2)
                pool.wait_ge(s_n2, TPB * (b + 1))
                pool.tensor_tensor(resid[:, TPB * b:TPB * b + TPB, :], resid[:, TPB * b:TPB * b + TPB, :],
                                   brow[:, 2:3, :].to_broadcast([P, TPB, D]), ALU.add).then_inc(s_xb2, 1)
                if b + 2 < B:
                    add_one(b + 2)
                if b == 1:
                    pool.wait_ge(s_tv_ev, t_unit(B - 1, HP - 1) + 1)
                    pool.memset(wk_g[:, :], 0.0).then_inc(s_qfree, 1)
                if b >= 2:
                    pass

            def split_q(b):
                pool.wait_ge(s_misc_ev, misc_at[("q", b)] + 1)
                if b >= 1:
                    pool.wait_ge(s_qst[(b - 1) % 2], 16 * 12 * ((b - 1) // 2 + 1))
                split([q_part[:, i, :] for i in range(3)], q_f[:, :], q_r[:, :], s_qpart)

            def split_m(b):
                pool.wait_ge(s_misc_ev, misc_at[("mT", b)] + 1)
                if b >= 1:
                    pool.wait_ge(s_mst[(b - 1) % 2], 16 * 6 * ((b - 1) // 2 + 1))
                split([m_part[:, i, :] for i in range(3)], m_f[:, :], m_r[:, :], s_mpart)

            split_q(0)
            split_q(1)
            split_m(0)
            for b in range(B):
                if b >= 1:
                    norm_batch(2, b - 1, s_mv3, s_n3)
                if b + 2 < B:
                    split_q(b + 2)
                if b + 1 < B:
                    split_m(b + 1)
            norm_batch(2, B - 1, s_mv3, s_n3)

        @block.tensor
        def _(pe):
            pe.wait_ge(s_const, 4)
            for t in range(NT):
                pe.wait_ge(s_n1, t + 1)
                last = pe.transpose(ps[:, 6 + t // 4, P * (t % 4):P * (t % 4) + P], norm[:, t, :], ident[:, :])
                if t % 4 == 3:
                    last.then_inc(s_set, 1)
            for i in range(4):
                pe.wait_ge(s_wprep, 2 * i + 2)
                for hh in (2 * i, 2 * i + 1):
                    last = pe.matmul(ps[:, i, 256 * (hh % 2):256 * (hh % 2) + 256], w_nat[:, hh, 0, :],
                                     wk_blk[:, hh, :], start=True, stop=True)
                last.then_inc(s_set, 1)
            for h in range(H):
                last = pe.matmul(ps[:, 4, h:h + 1], wk_blk[:, h // 2, D * (h % 2):D * (h % 2) + D],
                                 b_nat[:, h // 2, 0:1], start=True, stop=True)
            last.then_inc(s_set, 1)
            pe.wait_ge(s_wprep, 9)
            for hh in range(HP):
                if hh == 4:
                    pe.wait_ge(s_set_ev, 1)
                last = pe.transpose(ps[:, 5 + hh // 4, P * (hh % 4):P * (hh % 4) + P], wv_c[:, hh, :], ident[:, :])
                if hh % 4 == 3:
                    last.then_inc(s_set, 1)

            def t_of(b, u):
                k = t_unit(b, u)
                if k < 2:
                    pe.wait_ge(s_set_ev, 7)
                else:
                    pe.wait_ge(s_tv_ev, k - 1)
                for h in (2 * u, 2 * u + 1):
                    last = pe.matmul(ps[:, 3 + k % 2, S * (h % 2):S * (h % 2) + S], G[:, h, :],
                                     normT[:, S * b:S * b + S], start=True, stop=True)
                last.then_inc(s_tv, 1)

            for u in range(HP):
                t_of(0, u)
            pe.wait_ge(s_wo, 16)
            for c in range(HP):
                if c == 0:
                    pe.wait_ge(s_set_ev, 9)
                last = pe.transpose(ps[:, (7, 0)[c // 4], P * (c % 4):P * (c % 4) + P],
                                    wo_nat[:, P * c:P * c + P], ident[:, :])
                if c % 4 == 3:
                    last.then_inc(s_set, 1)
            pe.wait_ge(s_ctx, 16)
            for t in range(NT):
                last = pe.transpose(ps[:, 5 + t // 4, P * (t % 4):P * (t % 4) + P], ctx_nat[:, t, :], ident[:, :])
                if t % 4 == 3:
                    last.then_inc(s_set, 1)
            pe.wait_ge(s_wx, 144)
            pe.wait_ge(s_const, 9)
            for i in range(2):
                pe.wait_ge(s_set_ev, 12 + i)
                pe.matmul(ps[:, 1 + i, :], wqk[:, 1, :], ctxT[:, 512 * i:512 * i + 512],
                          start=True, stop=True).then_inc(s_set, 1)
            for t in range(NT):
                last = pe.matmul(ps[:, 5 + t // 4, P * (t % 4):P * (t % 4) + P], ctxT[:, P * t:P * t + P],
                                 wx[:, 2, :], start=True, stop=True)
                if t % 4 == 3:
                    last.then_inc(s_vx, 1)

            def scores(b, u):
                k = 12 * b + u
                if k == 0:
                    pe.wait_ge(s_set_ev, 15)
                ge(pe, s_exp, k - 2)
                if u == 0:
                    pe.wait_ge(s_nk, b + 1)
                bank = ps[:, k % 3, :]
                if u < HP:
                    pe.wait_ge(s_tv_ev, t_unit(b, u) + 1)
                    pe.matmul(bank, nk[:, b % 2, 0:P], t_sb[:, b % 2, 2 * u:2 * u + 2, :], start=True, stop=False)
                    pe.matmul(bank.rearrange("p (h q) -> p h q", h=2)[:, :, 0:P], ident_b[:, :], mask[:, 0:2, :],
                              start=False, stop=True).then_inc(s_sc, 1)
                else:
                    g = 4 * (u - HP)
                    pe.matmul(bank, nk[:, b % 2, P:S], t_sb[:, b % 2, g:g + 4, P:S], start=True, stop=False)
                    pe.matmul(bank, ident_b[:, :], mask[:, :, :], start=False, stop=True).then_inc(s_sc, 1)

            def values(b, u):
                k = v_unit(b, u)
                pe.wait_ge(s_tv_ev, k - 1)
                kt, hf = u // 2, u % 2
                pe.matmul(ps[:, 3 + k % 2, :], nk[:, b % 2, P * kt:P * kt + P], wvT[:, 512 * hf:512 * hf + 512],
                          start=True, stop=True).then_inc(s_tv, 1)

            def heads_out(b, zu):
                if b == 0 and zu < 2:
                    pe.wait_ge(s_vx_ev, 2)
                ge(pe, s_z_ev, 4 * b + zu - 1)
                if zu == 0:
                    pe.wait_ge(s_exp, 12 * b + 12)
                    pe.wait_ge(s_tv_ev, v_unit(b, 3) + 1)
                for pair in (2 * zu, 2 * zu + 1):
                    c0 = S * (pair % 2)
                    for kt in range(2):
                        for hp in range(2):
                            h = 2 * pair + hp
                            v = v_sb[:, kt, E1 * h:E1 * h + E1]
                            o = ps[64 * hp:64 * hp + 64, 5 + zu % 2, c0:c0 + S]
                            if kt == 0:
                                last = pe.matmul(o, v, p0[:, h, :], start=True, stop=False)
                            else:
                                last = pe.matmul(o[:, P:S], v, p1[:, h, :], start=False, stop=True)
                last.then_inc(s_z, 1)

            def project(b):
                if b == 0:
                    pe.wait_ge(s_set_ev, 11)
                ge(pe, s_x1, b)
                pe.wait_ge(s_z_ev, 4 * b + 4)
                for i in range(TPB):
                    for c in range(HP):
                        last = pe.matmul(ps[:, 7, P * i:P * i + P], zT[:, c, P * i:P * i + P], woT[:, c, :],
                                         start=(c == 0), stop=(c == HP - 1))
                last.then_inc(s_wo1, 1)

            for b in range(B):
                for u in range(12):
                    scores(b, u)
                    if u < HP and b + 1 < B:
                        t_of(b + 1, u)
                for u in range(4):
                    values(b, u)
                for zu in range(4):
                    heads_out(b, zu)
                project(b)

            def misc(key):
                n = misc_at[key]
                if n == 0:
                    pe.wait_ge(s_x1, B)
                ge(pe, s_misc_ev, n)

            def query(b):
                misc(("n2T", b))
                pe.wait_ge(s_n2, TPB * (b + 1))
                for i in range(TPB):
                    last = pe.transpose(ps[:, 7, P * i:P * i + P], norm[:, TPB * b + i, :], ident[:, :])
                last.then_inc(s_misc, 1)
                misc(("q", b))
                pe.matmul(ps[:, 7, 0:S], wqk[:, 0, :], n2T[:, :], start=True, stop=True).then_inc(s_misc, 1)

            def max_scores(b, u):
                g, qt = u // 2, u % 2
                if u == 0:
                    pe.wait_ge(s_qst[b % 2], 16 * 12 * (b // 2 + 1))
                    if b == 0:
                        pe.wait_ge(s_kst, 16 * 24)
                        pe.wait_ge(s_tv_ev, v_unit(B - 1, 3) + 1)
                        pe.wait_ge(s_z_ev, 4 * B)
                ge(pe, s_mx_ev, 16 * b + u - 1)
                for par in range(2):
                    last = pe.matmul(ps[:, 4 + u % 2, S * par:S * par + S],
                                     q_st[:, b % 2, g, S * par + P * qt:S * par + P * qt + P],
                                     k_max[:, g, S * b:S * b + S], start=True, stop=True)
                last.then_inc(s_mx, 1)

            def max_turn(b):
                misc(("mT", b))
                pe.wait_ge(s_mx_ev, 16 * b + 16)
                for i in range(TPB):
                    last = pe.transpose(ps[0:H, 7, P * i:P * i + P], mneg[:, i, :], ident[:, :])
                last.then_inc(s_misc, 1)

            def cross_scores(b, g):
                k = HP * b + g
                if g == 0:
                    pe.wait_ge(s_mst[b % 2], 16 * 6 * (b // 2 + 1))
                    if b == 0:
                        pe.wait_ge(s_exp, 12 * B)
                ge(pe, s_px, k - 1)
                for kt in range(2):
                    last = pe.matmul(ps[:, 2 * (k % 2) + kt, :],
                                     k_exp[:, g, S * b + P * kt:S * b + P * kt + P], q_st[:, b % 2, g, :],
                                     start=True, stop=True)
                last.then_inc(s_st, 1)

            def cross_out(b, g4):
                pe.wait_ge(s_px, HP * b + 2 * g4 + 2)
                if g4 % 2 == 0:
                    ge(pe, s_pv_ev, 2 * b + g4 // 2)
                    if b == 0 and g4 == 0:
                        pe.wait_ge(s_z_ev, 4 * B)
                for kt in range(2):
                    for j in range(4):
                        h = 2 * g4 + j // 2 + 8 * (j % 2)
                        p = px[:, g4 % 2, 1024 * (j // 2) + 512 * kt + S * (j % 2):][:, 0:S]
                        last = pe.matmul(ps[32 * j:32 * j + 32, 6, S * (g4 % 2):S * (g4 % 2) + S],
                                         v_pad[:, TPB * b + kt, h, :], p, start=(kt == 0), stop=(kt == 1))
                last.then_inc(s_pv, 1)

            def out_step(b, n):
                if n in (0, 2):
                    qt = n // 2
                    misc((f"oq{qt}", b))
                    pe.wait_ge(s_pv_ev, 2 * b + 2)
                    for g4 in range(4):
                        last = pe.transpose(ps[:, 7, P * g4:P * g4 + P], o_raw[:, g4, P * qt:P * qt + P], ident[:, :])
                elif n in (1, 3):
                    qt = n // 2
                    misc((f"oT{qt}", b))
                    last = pe.transpose(ps[:, 7, 0:P], o_n[:, qt, :], ident[:, :])
                else:
                    misc(("wo", b))
                    for i in range(TPB):
                        last = pe.matmul(ps[:, 7, P * i:P * i + P], oT[:, P * i:P * i + P], wx[:, 3, :],
                                         start=True, stop=True)
                last.then_inc(s_misc, 1)

            query(0)
            query(1)
            for u in range(16):
                max_scores(0, u)
            max_turn(0)
            for b in range(B):
                for g in range(HP):
                    cross_scores(b, g)
                    if g % 2 == 1 and g >= 3:
                        cross_out(b, g // 2 - 1)
                    if b + 1 < B:
                        max_scores(b + 1, 2 * g)
                        max_scores(b + 1, 2 * g + 1)
                    if b >= 1 and g < 5:
                        out_step(b - 1, g)
                cross_out(b, 3)
                if b + 2 < B:
                    query(b + 2)
                if b + 1 < B:
                    max_turn(b + 1)
            for n in range(5):
                out_step(B - 1, n)

            for t in range(NT):
                pe.wait_ge(s_n3, t + 1)
                last = pe.transpose(ps[:, t // 4, P * (t % 4):P * (t % 4) + P], norm[:, t, :], ident[:, :])
                if t % 4 == 3:
                    last.then_inc(s_rt, 1)
            pe.wait_ge(s_ffnb, 96)
            pe.transpose(ps[:, 2, 0:NE * NC], b1_nat[:, :], ident[0:NE * NC, 0:NE * NC]).then_inc(s_rt, 1)
            for t in range(NT):
                if t % 4 == 0:
                    pe.wait_ge(s_n3T, t // 4 + 1)
                last = pe.matmul(ps[:, 3, NE * t:NE * t + NE], normT[:, P * t:P * t + P], wr_sb[:, :],
                                 start=True, stop=True)
            last.then_inc(s_rt, 1)

            def hidden(k, c):
                e, hf = k // 2, k % 2
                n = 4 * k + c
                if n == 0:
                    pe.wait_ge(s_w1, 16)
                if n < 4:
                    pe.wait_ge((s_n3T, s_n3T, s_n3T, s_score)[n], (1, 2, 3, 1)[n])
                else:
                    pe.wait_ge(s_ha if c % 2 == 0 else s_hd, 2 * (k - 1) + c // 2 + 1)
                pe.matmul(ps[:, c, :], w1_sb[:, e, P * c:P * c + P], normT[:, 512 * hf:512 * hf + 512],
                          start=True, stop=True).then_inc(s_h, 1)

            def combine(k):
                e = k // 2
                if k == 0:
                    pe.wait_ge(s_w2, 16)
                    pe.wait_ge(s_mx_ev, 16 * B)
                ge(pe, s_acc, k - 1)
                pe.wait_ge(s_ha, 2 * k + 2)
                pe.wait_ge(s_hd, 2 * k + 2)
                for tt in range(4):
                    for c in range(NC):
                        last = pe.matmul(ps[:, 4 + k % 2, P * tt:P * tt + P], hid[:, k % 2, c, P * tt:P * tt + P],
                                         w2_sb[:, NC * e + c, :], start=(c == 0), stop=(c == NC - 1))
                last.then_inc(s_y, 1)

            for c in range(NC):
                hidden(0, c)
            pe.wait_ge(s_wgt, 1)
            pe.wait_ge(s_pv_ev, 2 * B)
            for t in range(NT):
                last = pe.transpose(ps[0:NE, 6 + t // 4, P * (t % 4):P * (t % 4) + P], wgt[:, t, :], ident[:, :])
            last.then_inc(s_wT, 1)
            for c in range(NC):
                hidden(1, c)
            pe.wait_ge(s_wTe, 1)
            for t in range(NT):
                last = pe.matmul(ps[:, 6 + t // 4, P * (t % 4):P * (t % 4) + P], wgtT[:, P * t:P * t + P],
                                 b2_sb[:, :], start=True, stop=True)
            last.then_inc(s_b2, 1)
            combine(0)
            for k in range(2, 2 * NE):
                for c in range(NC):
                    hidden(k, c)
                combine(k - 1)
            combine(2 * NE - 1)

        @block.scalar
        def _(act):
            act.dma_start(wo_nat, w_o).then_inc(s_wo, 16)
            act.dma_start(ctx_nat, ctx_in.rearrange(tiles, p=P)).then_inc(s_ctx, 16)
            for i, w in enumerate((wq, wk, wv, wo)):
                act.dma_start(wx[:, i, :], w).then_inc(s_wx, 16)
            with nc.allow_non_contiguous_dma(reason="128 biases, in the order of the permuted columns"):
                for i, v in enumerate((bq, bk)):
                    for par in range(2):
                        act.dma_start(bqk[64 * par:64 * par + 64, i:i + 1],
                                      v[64 * par:64 * par + 64].rearrange("(g d) -> d g", d=DH)).then_inc(s_ffnb, 16)
            for i, v in enumerate((b_o, bv, bo)):
                act.dma_start(brow[:, i, :], v.partition_broadcast(P)).then_inc(s_wx, 16)
            act.dma_start(br_row[:, :], br.partition_broadcast(P)).then_inc(s_wx, 16)
            act.dma_start(wr_sb[:, :], wr).then_inc(s_wx, 16)
            act.dma_start(b1_nat[:, :], b1.rearrange("e (c p) -> (e c) p", p=P)).then_inc(s_ffnb, 16)
            act.dma_start(b2_sb[:, :], b2).then_inc(s_ffnb, 16)

            def copy_out(n, dst, src):
                act.wait_ge(s_set, n + 1)
                act.copy(dst, src).then_inc(s_set_ev, 1)

            for i in range(2):
                copy_out(i, normT[:, 512 * i:512 * i + 512], ps[:, 6 + i, :])
            for i in range(4):
                copy_out(2 + i, G[:, 4 * i:4 * i + 4, :], ps[:, i, :])
            copy_out(6, cvec[:, :], ps[:, 4, 0:H])
            for i in range(2):
                copy_out(7 + i, wvT[:, 512 * i:512 * i + 512], ps[:, 5 + i, :])
            for i in range(2):
                copy_out(9 + i, woT[:, 4 * i:4 * i + 4, :], ps[:, (7, 0)[i], :])
            for i in range(2):
                copy_out(11 + i, ctxT[:, 512 * i:512 * i + 512], ps[:, 5 + i, :])
            act.wait_ge(s_ffnb, 96)
            for i in range(2):
                act.wait_ge(s_set, 14 + i)
                act.activation(k_f[:, 512 * i:512 * i + 512], ps[:, 1 + i, :], ACT.Identity,
                               bias=bqk[:, 1:2]).then_inc(s_set_ev, 1)

            def probabilities(b, u):
                k = 12 * b + u
                act.wait_ge(s_max, k + 1)
                bank = ps[:, k % 3, :]
                if u < HP:
                    heads, kt, n = range(2 * u, 2 * u + 2), 0, S
                else:
                    heads, kt, n = range(4 * (u - HP), 4 * (u - HP) + 4), 1, P
                for i, h in enumerate(heads):
                    dst = p0[:, h, :] if kt == 0 else p1[:, h, :]
                    last = act.activation(dst, bank[:, n * i:n * i + n], ACT.Exp, bias=negmax[:, kt, h:h + 1],
                                          accum_out=psums[:, kt, h:h + 1])
                last.then_inc(s_exp, 1)

            for b in range(B):
                if b == 0:
                    act.wait_ge(s_kpart, 3)
                for u in range(12):
                    probabilities(b, u)
                for zu in range(4):
                    act.wait_ge(s_z, 4 * b + zu + 1)
                    act.copy(zT[:, 2 * zu:2 * zu + 2, :], ps[:, 5 + zu % 2, :]).then_inc(s_z_ev, 1)

            def query_out(b):
                act.wait_ge(s_misc, misc_at[("n2T", b)] + 1)
                act.copy(n2T[:, :], ps[:, 7, 0:S]).then_inc(s_misc_ev, 1)
                act.wait_ge(s_misc, misc_at[("q", b)] + 1)
                ge(act, s_qpart, 3 * b)
                act.activation(q_f[:, :], ps[:, 7, 0:S], ACT.Identity, bias=bqk[:, 0:1]).then_inc(s_misc_ev, 1)

            def max_out(b):
                act.wait_ge(s_misc, misc_at[("mT", b)] + 1)
                ge(act, s_mpart, 3 * b)
                act.copy(m_f[:, :], ps[0:H, 7, 0:S]).then_inc(s_misc_ev, 1)

            def cross_probabilities(b, g):
                k = HP * b + g
                act.wait_ge(s_st, k + 1)
                ge(act, s_pv, 4 * b + g // 2 - 1)
                act.activation(px[:, (g // 2) % 2, 1024 * (g % 2):1024 * (g % 2) + 1024],
                               ps[:, 2 * (k % 2):2 * (k % 2) + 2, :].rearrange("p a n -> p (a n)"), ACT.Exp,
                               scale=SCALE_X).then_inc(s_px, 1)

            def cross_copy(b, i):
                act.wait_ge(s_pv, 4 * b + 2 * i + 2)
                if i == 0:
                    ge(act, s_misc, misc_at[("oq1", b - 1)] + 1 if b else 0)
                act.copy(o_raw[:, 2 * i:2 * i + 2, :], ps[:, 6, :]).then_inc(s_pv_ev, 1)

            def out_copy(b, qt):
                act.wait_ge(s_misc, misc_at[(f"oT{qt}", b)] + 1)
                act.copy(oT[:, P * qt:P * qt + P], ps[:, 7, 0:P]).then_inc(s_misc_ev, 1)

            query_out(0)
            query_out(1)
            max_out(0)
            for b in range(B):
                for g in range(HP):
                    cross_probabilities(b, g)
                    if g == 6:
                        cross_copy(b, 0)
                    if b >= 1 and g in (1, 3):
                        out_copy(b - 1, g // 2)
                cross_copy(b, 1)
                if b + 2 < B:
                    query_out(b + 2)
                if b + 1 < B:
                    max_out(b + 1)
            for qt in range(2):
                out_copy(B - 1, qt)

            for i in range(2):
                act.wait_ge(s_rt, i + 1)
                act.copy(normT[:, 512 * i:512 * i + 512], ps[:, i, :]).then_inc(s_n3T, 1)
            act.wait_ge(s_rt, 3)
            act.copy(b1T[:, :], ps[:, 2, 0:NE * NC]).then_inc(s_n3T, 1)
            act.wait_ge(s_score, 2)
            act.activation(gate[:, 1, :], gate[:, 0, :], ACT.Exp).then_inc(s_ed, 1)
            act.wait_ge(s_n3T, 3)
            for k in range(2 * NE):
                for c in (0, 2):
                    act.wait_ge(s_h, 4 * k + c + 1)
                    ge(act, s_y, k - 1)
                    act.activation(hid[:, k % 2, c, :], ps[:, c, :], ACT.Relu,
                                   bias=b1T[:, NC * (k // 2) + c:NC * (k // 2) + c + 1]).then_inc(s_ha, 1)
                if k == 0:
                    act.wait_ge(s_wT, 1)
                    act.copy(wgtT[:, :].rearrange("p (a n) -> p a n", a=2), ps[0:NE, 6:8, :]).then_inc(s_wTe, 1)

        @block.vector
        def _(dve):
            steps = [0]

            def step(ins):
                steps[0] += 1
                ins.then_inc(s_dve, 1)
                dve.wait_ge(s_dve, steps[0])

            dve.wait_ge(s_x, 16)
            for t in range(NT):
                dve.bn_stats(stats[:, t, :], resid[:, t, :]).then_inc(s_bn, 1)
            dve.wait_ge(s_bn, NT)
            for t in range(NT):
                dve.bn_aggr(mv[:, 0, t, :], stats[:, t, :]).then_inc(s_mv, 1)
            dve.wait_ge(s_rstd, 1)
            for t in range(NT):
                dve.tensor_scalar(norm[:, t, :], resid[:, t, :], negm[:, 0, t:t + 1], rstd[:, 0, t:t + 1],
                                  ALU.add, ALU.mult).then_inc(s_n1, 1)
            dve.wait_ge(s_bias, 16)
            dve.wait_ge(s_const, 3)
            for i in range(4):
                dve.wait_ge(s_w[i], 16)
                hs = slice(2 * i, 2 * i + 2)
                step(dve.tensor_reduce(row_add[:, :, hs].rearrange("p c h -> p h c"), w_nat[:, hs, 1:3, :], AX, ALU.add))
                step(dve.tensor_tensor(row_add[:, :, hs].rearrange("p c h -> p h c"), b_nat[:, hs, 1:3],
                                       row_add[:, :, hs].rearrange("p c h -> p h c"), ALU.subtract))
                step(dve.tensor_scalar(row_add[:, :, hs], row_add[:, :, hs], 1.0 / D, None, ALU.mult))
                for hp in range(2):
                    r = slice(64 * hp, 64 * hp + 64)
                    dve.tensor_tensor(wk_blk[r, hs, D * hp:D * hp + D], w_nat[r, hs, 1, :],
                                      row_add[r, 0, hs].unsqueeze(2).to_broadcast([64, 2, D]), ALU.add
                                      ).then_inc(s_wprep, 1)
            dve.tensor_tensor(wv_c, w_nat[:, :, 2, :], row_add[:, 1, :].unsqueeze(2).to_broadcast([P, HP, D]),
                              ALU.add).then_inc(s_wprep, 1)

            def t_out(b, u):
                k = t_unit(b, u)
                dve.wait_ge(s_tv, k + 1)
                if k == 0:
                    dve.wait_ge(s_set_ev, 7)
                dve.tensor_tensor(t_sb[:, b % 2, 2 * u:2 * u + 2, :],
                                  ps[:, 3 + k % 2, :].rearrange("p (h q) -> p h q", h=2),
                                  cvec[:, 2 * u:2 * u + 2].unsqueeze(2).to_broadcast([P, 2, S]), ALU.add
                                  ).then_inc(s_tv_ev, 1)

            for u in range(HP):
                t_out(0, u)
            for i in range(2):
                dve.wait_ge(s_vx, i + 1)
                dve.wait_ge(s_wx, 144)
                dve.wait_ge(s_const, 7)
                dve.tensor_tensor(v_pad[:, 4 * i:4 * i + 4, :, 0:DH],
                                  ps[:, 5 + i, :].rearrange("p (t h d) -> p t h d", t=4, h=H),
                                  brow[:, 1, :].rearrange("p (h d) -> p h d", d=DH).unsqueeze(1).to_broadcast([P, 4, H, DH]),
                                  ALU.add).then_inc(s_vx_ev, 1)

            def maxima(b, u):
                k = 12 * b + u
                dve.wait_ge(s_sc, k + 1)
                if u < HP:
                    dst, n = negmax[:, 0, 2 * u:2 * u + 2], 2
                else:
                    dst, n = negmax[:, 1, 4 * (u - HP):4 * (u - HP) + 4], 4
                dve.tensor_reduce(dst, ps[:, k % 3, :].rearrange("p (h q) -> p h q", h=n), AX, ALU.max,
                                  negate=True).then_inc(s_max, 1)

            def values_out(b, u):
                kt, hf = u // 2, u % 2
                dve.wait_ge(s_exp, 12 * b + (4 * (hf + 1) if kt == 0 else HP + 2 * (hf + 1)))
                hs = slice(8 * hf, 8 * hf + 8)
                step(dve.reciprocal(rsum[:, kt, hs], psums[:, kt, hs]))
                k = v_unit(b, u)
                dve.wait_ge(s_tv, k + 1)
                if b == 0 and u == 0:
                    dve.wait_ge(s_kpart, 3)
                dve.tensor_tensor(v_sb[:, kt, 512 * hf:512 * hf + 512].rearrange("p (h e) -> p h e", e=E1),
                                  ps[:, 3 + k % 2, :].rearrange("p (h e) -> p h e", e=E1),
                                  rsum[:, kt, hs].unsqueeze(2).to_broadcast([P, 8, E1]), ALU.mult).then_inc(s_tv_ev, 1)

            def residual(n, b, s_done, count, s_stat):
                ts = slice(TPB * b, TPB * b + TPB)
                dve.tensor_tensor(resid[:, ts, :], ps[:, 7, 0:S].rearrange("p (t d) -> p t d", d=D),
                                  resid[:, ts, :], ALU.add).then_inc(s_done, 1)
                dve.wait_ge(s_done, count)
                for t in range(TPB * b, TPB * b + TPB):
                    step(dve.bn_stats(stats[:, t, :], resid[:, t, :]))
                    dve.bn_aggr(mv[:, n, t, :], stats[:, t, :]).then_inc(s_stat, 1)

            for b in range(B):
                for u in range(12):
                    maxima(b, u)
                    if u < HP and b + 1 < B:
                        t_out(b + 1, u)
                for u in range(4):
                    values_out(b, u)
                dve.wait_ge(s_wo1, b + 1)
                if b == 0:
                    dve.wait_ge(s_xb, 1)
                residual(1, b, s_x1, b + 1, s_mv2)

            def cross_max(b, u):
                g, qt = u // 2, u % 2
                dve.wait_ge(s_mx, 16 * b + u + 1)
                if u == 0 and b >= 1:
                    dve.wait_ge(s_misc, misc_at[("mT", b - 1)] + 1)
                dve.tensor_reduce(mneg[:, qt, :].rearrange("p (r g) -> p r g", r=2)[:, :, g],
                                  ps[:, 4 + u % 2, :].rearrange("p (h k) -> p h k", h=2), AX, ALU.max,
                                  negate=True).then_inc(s_mx_ev, 1)

            def cross_normalise(b, qt):
                dve.wait_ge(s_misc, misc_at[(f"oq{qt}", b)] + 1)
                turned = ps[:, 7, :].rearrange("p (g j r) -> p g j r", g=4, j=4)
                step(dve.reciprocal(r_den[:, qt, :].rearrange("p (g j) -> p g j", g=4), turned[:, :, :, DH]))
                for par in range(2):
                    src = turned[:, :, :, :].rearrange("p g (a r) c -> p g a r c", r=2)[:, :, :, par, 0:DH]
                    den = r_den[:, qt, :].rearrange("p (g a r) -> p g a r", g=4, r=2)[:, :, :, par]
                    last = (dve.tensor_tensor(o_n[:, qt, 64 * par:64 * par + 64].rearrange("p (g a d) -> p g a d", g=4, d=DH),
                                           src, den.unsqueeze(3).to_broadcast([P, 4, 2, DH]), ALU.mult))
                last.then_inc(s_misc_ev, 1)

            def cross_residual(b):
                dve.wait_ge(s_misc, misc_at[("wo", b)] + 1)
                dve.wait_ge(s_xb2, b + 1)
                residual(2, b, s_misc_ev, misc_at[("wo", b)] + 1, s_mv3)

            for u in range(16):
                cross_max(0, u)
            for b in range(B):
                for g in range(HP):
                    if b + 1 < B:
                        cross_max(b + 1, 2 * g)
                        cross_max(b + 1, 2 * g + 1)
                    if b >= 1 and g in (0, 2):
                        cross_normalise(b - 1, g // 2)
                    if b >= 1 and g == 4:
                        cross_residual(b - 1)
            for qt in range(2):
                cross_normalise(B - 1, qt)
            cross_residual(B - 1)

            dve.wait_ge(s_rt, 4)
            dve.tensor_tensor(score[:, :, :], ps[:, 3, 0:NT * NE].rearrange("p (t e) -> p t e", e=NE),
                              br_row[:, :].unsqueeze(1).to_broadcast([P, NT, NE]), ALU.add).then_inc(s_score, 1)
            dve.wait_ge(s_score, 1)
            for t in range(NT):
                step(dve.max(top[:, t, :], score[:, t, :]))
                step(dve.max_index(top_i[:, t, :], top[:, t, :], score[:, t, :]))
            dve.tensor_tensor(gate[:, 0, :], top[:, :, 1], top[:, :, 0], ALU.subtract).then_inc(s_score, 1)
            step(dve.tensor_copy(top_f[:, :, :], top_i[:, :, 0:2]))
            for n in range(2):
                step(dve.tensor_tensor(hot[:, n, :, :], iota8[:, :].unsqueeze(1).to_broadcast([P, NT, NE]),
                                       top_f[:, :, n:n + 1].to_broadcast([P, NT, NE]), ALU.is_equal))
            dve.wait_ge(s_ed, 1)
            step(dve.tensor_scalar(gate[:, 2, :], gate[:, 1, :], 1.0, None, ALU.add))
            step(dve.reciprocal(gate[:, 2, :], gate[:, 2, :]))
            step(dve.tensor_tensor(gate[:, 3, :], gate[:, 1, :], gate[:, 2, :], ALU.mult))
            for n in range(2):
                step(dve.tensor_tensor(hot[:, n, :, :], hot[:, n, :, :],
                                       gate[:, 2 + n, :].unsqueeze(2).to_broadcast([P, NT, NE]), ALU.mult))
            dve.tensor_tensor(wgt[:, :, :], hot[:, 0, :, :], hot[:, 1, :, :], ALU.add).then_inc(s_wgt, 1)
            dve.wait_ge(s_n3T, 3)

            def relu(k, c):
                dve.wait_ge(s_h, 4 * k + c + 1)
                ge(dve, s_y, k - 1)
                dve.tensor_scalar(hid[:, k % 2, c, :], ps[:, c, :], b1T[:, NC * (k // 2) + c:NC * (k // 2) + c + 1],
                                  0.0, ALU.add, ALU.max).then_inc(s_hd, 1)

            def accumulate(k):
                e, hf = k // 2, k % 2
                dve.wait_ge(s_y, k + 1)
                ge(dve, s_acc, k - 1)
                for tt in range(4):
                    t = 4 * hf + tt
                    last = dve.scalar_tensor_tensor(resid[:, t, :], ps[:, 4 + k % 2, P * tt:P * tt + P],
                                                    wgt[:, t, e:e + 1], resid[:, t, :], ALU.mult, ALU.add)
                last.then_inc(s_acc, 1)

            for k in range(2 * NE):
                relu(k, 1)
                relu(k, 3)
                if k == 1:
                    dve.wait_ge(s_b2, 1)
                    dve.wait_ge(s_wgt, 1)
                    dve.wait_ge(s_n3, NT)
                    dve.tensor_tensor(resid[:, :, :], ps[:, 6:8, :].rearrange("p a (t d) -> p (a t) d", d=D),
                                      resid[:, :, :], ALU.add).then_inc(s_acc0, 1)
                    dve.wait_ge(s_acc0, 1)
                if k >= 1:
                    accumulate(k - 1)
            accumulate(2 * NE - 1)


_INS = ['x', 'ctx_1024', 'L0_attn_W_qkv', 'L0_attn_b_qkv', 'L0_attn_W_o', 'L0_attn_b_o',
        'L0_xattn_Wq', 'L0_xattn_bq', 'L0_xattn_Wk', 'L0_xattn_bk', 'L0_xattn_Wv', 'L0_xattn_bv',
        'L0_xattn_Wo', 'L0_xattn_bo', 'L0_ffn_Wr', 'L0_ffn_br', 'L0_ffn_W1', 'L0_ffn_b1', 'L0_ffn_W2', 'L0_ffn_b2']


def kernel(**inputs):
    import numpy as _np
    import concourse.bacc as _bacc
    from concourse import mybir as _mybir
    from concourse.bass_utils import run_bass_kernel_spmd as _run

    nc = _bacc.Bacc("TRN2", target_bir_lowering=False, num_devices=1)
    arrays, args = {}, []
    for name in _INS:
        a = _np.ascontiguousarray(inputs[name])
        arrays[f"in_{name}"] = a
        args.append(nc.dram_tensor(f"in_{name}", a.shape, _mybir.dt.from_np(a.dtype), kind="ExternalInput").ap())
    shape = arrays["in_x"].shape
    args.append(nc.dram_tensor("out_dram", shape, _mybir.dt.float32, kind="ExternalOutput").ap())
    decoder_layer(nc, *args)
    r = _run(nc, [arrays], core_ids=[0])
    return r.results[0]["out_dram"]
```

```python
from contextlib import ExitStack

import concourse.bass as bass
from concourse import mybir

F32 = mybir.dt.float32
F32R = mybir.dt.float32r
BF16 = mybir.dt.bfloat16
U32 = mybir.dt.uint32
ALU = mybir.AluOpType
ACT = mybir.ActivationFunctionType
AX = mybir.AxisListType.X

P = 128
B, S, D = 4, 256, 128
NT = B * S // P
TPB = S // P
H, E1 = 16, 64
HP = H // 2
DH = 8
NE, HID = 8, 512
NC = HID // P
EPS_LN, EPS_RMS = 1e-5, 1.1920929e-07
MASKED = -1.0e38
PARTS_Q = (0, 0, 0, 1, 1, 2)
PARTS_K = (0, 1, 2, 0, 1, 0)
MAX_ROW = DH * len(PARTS_Q)
TWO_ONES = 1.0 + 0x3F80 / 2.0 ** 23
SCALE_X = float(DH) ** -0.5


def ge(eng, sem, value):
    if value > 0:
        eng.wait_ge(sem, value)


def decoder_layer(nc, x, ctx_in, w_qkv, b_qkv, w_o, b_o, wq, bq, wk, bk, wv, bv, wo, bo,
                  wr, br, w1, b1, w2, b2, out):
    ctx = ExitStack()
    with ctx:
        def sb(name, shape, dt=F32):
            return ctx.enter_context(nc.sbuf_tensor(name, shape, dt))

        def sem(name):
            return ctx.enter_context(nc.semaphore(name))

        resid = sb("resid", [P, NT, D])

        def overlay(*layouts):
            made = []
            for n, layout in enumerate(layouts):
                kept = ctx if n == len(layouts) - 1 else ExitStack()
                made += [kept.enter_context(nc.sbuf_tensor(name, [P, cols], dt)) for name, cols, dt in layout]
                if kept is not ctx:
                    kept.close()
            return made

        w_in, q_mem0, hid = overlay([("w_in", 4096, F32)], [("q_mem0", 8192, BF16)], [("hid", 4096, F32)])
        hid = hid[:, :].rearrange("p (r c n) -> p r c n", r=2, c=NC)
        w_nat = w_in[:, 0:3072].rearrange("p (hh c d) -> p hh c d", c=3, d=D)
        wv_c = w_in[:, 3072:4096].rearrange("p (hh d) -> p hh d", d=D)
        wk_mem, g_hi, ctxT, k_f, q_mem1 = overlay(
            [("wk_blk", 2048, F32), ("g_hi", 2048, F32R)], [("ctxT", 1024, F32), ("k_f", 1024, F32)],
            [("q_mem1", 8192, BF16)])
        wk_blk = wk_mem[:, :].rearrange("p (hh n) -> p hh n", n=2 * D)
        q_mem = [q_mem0, q_mem1]
        q_st = [q_mem[b // 2][:, :].rearrange("p (r g n) -> p r g n", r=2, g=HP)[:, b % 2] for b in range(B)]
        px, g_lo, t_hi, t_lo = overlay([("px", 4096, F32)], [("g_lo", 2048, F32R), ("t_hi", 3072, F32R), ("t_lo", 3072, F32R)])
        G = [w[:, :].rearrange("p (h n) -> p h n", n=D) for w in (g_hi, g_lo)]
        t_ring = [w[:, :].rearrange("p (h q) -> p h q", q=S) for w in (t_hi, t_lo)]
        px = px[:, :].rearrange("p (r n) -> p r n", r=2)
        wvT, v_sb, w1_hi = overlay([("wvT", 2048, F32R), ("v_sb", 2048, F32)], [("w1_hi", 4096, F32R)])
        wvT = wvT[:, :].rearrange("p (i n) -> p i n", i=2)
        v_sb = v_sb[:, :].rearrange("p (k n) -> p k n", k=2)
        p01, w1_lo, w1_raw, w2_raw = overlay([("p01", H * S + H * P + HP * S, F32)], [("w1_lo", 4096, F32R)],
                                             [("w1_raw", 4096, F32), ("w2_raw", 4096, F32)])
        p0 = p01[:, 0:H * S].rearrange("p (h q) -> p h q", h=H)
        p1 = p01[:, H * S:H * S + H * P].rearrange("p (h q) -> p h q", h=H)
        zT = p01[:, H * S + H * P:].rearrange("p (c q) -> p c q", c=HP)
        wo_nat = p01[:, 6144:7168]
        ctx_nat = p01[:, 7168:8192].rearrange("p (t d) -> p t d", d=D)
        w1_p = [w[:, :].rearrange("p (e n) -> p e n", n=HID) for w in (w1_hi, w1_lo)]
        w2_sb = w2_raw[:, :].rearrange("p (n d) -> p n d", d=D)
        b_nat = sb("b_nat", [P, HP, 3])
        b_q = sb("b_q", [P, HP])
        row_add = sb("row_add", [P, 2, HP])
        b_over_d = sb("b_over_d", [P, HP, 2])
        cvec = sb("cvec", [P, H])
        woT = sb("woT", [P, HP, D])
        n_parts = sb("n_parts", [P, 2, NT * P], F32R)
        negmax = sb("negmax", [P, 2, H])
        psums = sb("psums", [P, 2, H])
        rsum = sb("rsum", [P, 2, H])
        norm = sb("norm", [P, NT, D])
        stats = sb("stats", [P, NT, 6])
        mv = sb("mv", [P, 3, NT, 2])
        rstd = sb("rstd", [P, 3, NT])
        tmp8 = sb("tmp8", [P, 3, NT])
        negm = sb("negm", [P, 3, NT])
        k_part = sb("k_part", [P, 3, NT * P], BF16)
        k_st = sb("k_st", [P, HP, NT * P], BF16)
        v_pad = sb("v_pad", [P, NT, (DH + 1) * H + 32])
        v_heads = v_pad[:, :, 0:(DH + 1) * H].rearrange("p t (h d) -> p t h d", d=DH + 1)
        n2T = sb("n2T", [P, S])
        q_f = sb("q_f", [P, S])
        q_r = sb("q_r", [P, S])
        q_part = sb("q_part", [P, 3, S], BF16)
        mneg = sb("mneg", [P, TPB, H])
        m_f = sb("m_f", [H, S])
        m_r = sb("m_r", [H, S])
        m_part = sb("m_part", [H, 3, S], BF16)
        o_raw = sb("o_raw", [P, 4, S])
        k_r = o_raw[:, :, :].rearrange("p a n -> p (a n)")
        r_den = sb("r_den", [P, TPB, 16])
        o_n = sb("o_n", [P, TPB, D])
        oT = sb("oT", [P, S])
        wx = sb("wx", [P, 4, D])
        wqk = sb("wqk", [P, 2, D])
        bqk = sb("bqk", [P, 2])
        brow = sb("brow", [P, 3, D])
        wr_sb = sb("wr_sb", [P, NE])
        br_row = sb("br_row", [P, NE])
        b1_nat = sb("b1_nat", [NE * NC, P])
        b1T = sb("b1T", [P, NE * NC])
        b2_sb = sb("b2_sb", [NE, D])
        ident = sb("ident", [P, P])
        ident_b = sb("ident_b", [P, P], BF16)
        mask = sb("mask", [P, 4, P], BF16)
        half = sb("half", [P, NT])
        one = sb("one", [P, 1])
        score = sb("score", [P, NT, NE])
        top = sb("top", [P, NT, 8])
        top_i = sb("top_i", [P, NT, 8], U32)
        top_f = sb("top_f", [P, NT, 2])
        iota8 = sb("iota8", [P, NE])
        gate = sb("gate", [P, 4, NT])
        hot = sb("hot", [P, 2, NT, NE])
        wgt = sb("wgt", [P, NT, NE])
        wgtT = woT[0:NE, :, :].rearrange("p c d -> p (c d)")

        ps = ctx.enter_context(nc.psum_tensor("ps", [P, 8, 512], F32))

        s_x, s_bias, s_wo, s_ctx, s_wx, s_ffnb = (sem(n) for n in ("s_x", "s_bias", "s_wo", "s_ctx", "s_wx", "s_ffnb"))
        s_w = [sem(f"s_wqkv{i}") for i in range(4)]
        s_w12, s_out = [sem("s_w1"), sem("s_w2")], sem("s_out")
        s_const = sem("s_const")
        s_pool = sem("s_pool")
        s_dve = sem("s_dve")
        s_bn, s_mv, s_rstd, s_n1 = sem("s_bn"), sem("s_mv"), sem("s_rstd"), sem("s_n1")
        s_wprep = sem("s_wprep")
        s_set, s_set_ev, s_set_lo = sem("s_set"), sem("s_set_ev"), sem("s_set_lo")
        s_vx, s_vx_ev = sem("s_vx"), sem("s_vx_ev")
        s_xb = sem("s_xb")
        s_kpart, s_kst = sem("s_kpart"), sem("s_kst")
        s_sc, s_max, s_exp = sem("s_sc"), sem("s_max"), sem("s_exp")
        s_t, s_t_hi, s_t_lo = sem("s_t"), sem("s_t_hi"), sem("s_t_lo")
        s_v, s_v_ev = sem("s_v"), sem("s_v_ev")
        s_z, s_z_ev = sem("s_z"), sem("s_z_ev")
        s_mv2, s_n2, s_xb2 = sem("s_mv2"), sem("s_n2"), sem("s_xb2")
        s_misc, s_misc_ev = sem("s_misc"), sem("s_misc_ev")
        s_qpart, s_qfree = sem("s_qpart"), sem("s_qfree")
        s_qst = [sem(f"s_qst{b}") for b in range(B)]
        s_mst = [sem(f"s_mst{b}") for b in range(B)]
        s_mx, s_mx_ev, s_mpart = sem("s_mx"), sem("s_mx_ev"), sem("s_mpart")
        s_st, s_px, s_pv, s_pv_ev = sem("s_st"), sem("s_px"), sem("s_pv"), sem("s_pv_ev")
        s_mv3, s_n3 = sem("s_mv3"), sem("s_n3")
        s_whi, s_wlo = sem("s_whi"), sem("s_wlo")
        s_n3T, s_score, s_ed, s_wgt, s_b2 = sem("s_n3T"), sem("s_score"), sem("s_ed"), sem("s_wgt"), sem("s_b2")
        s_h, s_ha, s_hd, s_y, s_acc = sem("s_h"), sem("s_ha"), sem("s_hd"), sem("s_y"), sem("s_acc")

        tiles = "b (i p) d -> p (b i) d"

        slots = [[("T", 0, 0)], [("T", 0, 1)]]
        for b in range(B):
            tail = {0: [("V", b - 1, 2), ("V", b - 1, 3)], 2: [("Z", b - 1, 2)], 3: [("Z", b - 1, 3)], 4: [("PJ", b - 1)],
                    6: [("n2T", b - 1)], 8: [("q", b - 1)]} if b >= 1 else {}
            own = {3: [("T", b, 6)], 4: [("T", b, 7)], 5: [("V", b, 0)], 6: [("V", b, 1)], 8: [("Z", b, 0)], 9: [("Z", b, 1)]}
            if b >= 1:
                own[1], own[2] = [("T", b, 4)], [("T", b, 5)]
            else:
                own[0], own[1], own[2] = [("T", 0, 2)], [("T", 0, 3)], [("T", 0, 4), ("T", 0, 5)]
            ahead = {6: [("T", b + 1, 0)], 7: [("T", b + 1, 1)], 9: [("T", b + 1, 2)], 10: [("T", b + 1, 3)]} if b + 1 < B else {}
            for s in range(12):
                slot = [("S", b, s)]
                units = tail.get(s, []) + own.get(s, []) + ahead.get(s, [])
                if b == 0 and s < 10:
                    units += [("P", 0, s)]
                if b >= 2 and 3 <= s < 11:
                    units = [("MX", b - 2, 2 * (s - 3))] + units + [("MX", b - 2, 2 * (s - 3) + 1)]
                if b >= 2 and s == 11:
                    units += [("mT", b - 2)]
                slots.append(slot + units)
        last = B - 1
        max_plan = {(0, g): (2, 3 * (g - 3), 3) for g in range(3, 8)}
        max_plan.update({(1, 0): (2, 15, 1), (1, 6): (3, 0, 2), (1, 7): (3, 2, 2)})
        max_plan.update({(2, g): (3, 4 + 3 * g, 3) for g in range(4)})
        for b in range(B):
            outs = {2: [("oq0", b - 1)], 3: [("oT0", b - 1)], 4: [("oq1", b - 1)], 5: [("oT1", b - 1)], 6: [("wo", b - 1)]}
            tail = outs if b else {0: [("V", last, 2), ("V", last, 3)], 1: [("Z", last, 2)], 2: [("Z", last, 3)],
                                   3: [("PJ", last)], 5: [("n2T", last)], 6: [("q", last)]}
            more = {(1, 1): [("mT", 2)], (2, 4): [("mT", 3)], (2, 1): [("b1", 0)], (3, 1): [("NT", 0)], (3, 7): [("RT", 0)]}
            for g in range(HP):
                slot = [("CS", b, g)] + tail.get(g, []) + more.get((b, g), [])
                if g in (2, 4, 6):
                    slot += [("CO", b, g // 2 - 1)]
                if g == 0 and b >= 1:
                    slot += [("CO", b - 1, 3)]
                mb, m, n = max_plan.get((b, g), (0, 0, 0))
                slot += [("MX", mb, m + i) for i in range(n)]
                if b == 2:
                    slot += [("WS", 0, g)]
                slots.append(slot)
        slots.append([("CO", last, 3)])
        extra = {0: [("GT", 0), ("oq0", last)], 1: [("WT", 0), ("oT0", last)], 2: [("B2", 0), ("oq1", last)], 3: [("oT1", last), ("wo", last)],
                 5: [("NT", 1)], 6: [("RT", 1)], 7: [("GT", 1)], 8: [("WT", 1)], 9: [("B2", 1)]}
        for k in range(2 * NE):
            more = extra.get(k, []) + [None, None]
            units = [("H", k, 0), more[0], ("H", k, 1), ("H", k, 2), more[1], ("H", k, 3)]
            slots.append([u for u in units if u] + ([("Y", k - 1)] if k else []))
        slots.append([("Y", 2 * NE - 1)])
        MISC = ("PJ", "n2T", "q", "mT", "oq0", "oT0", "oq1", "oT1", "wo", "b1", "NT", "RT", "WT", "B2")
        misc_at = {k: i for i, k in enumerate(k for slot in slots for k in slot if k[0] in MISC)}
        ring = [k for slot in slots for k in slot if k[0] in "TVZ"]
        ring_bank = {k: 3 + i % 3 for i, k in enumerate(ring)}
        H_BANK, Y_BANK = (0, 1, 2, 5), (6, 3)

        flat = [k for slot in slots for k in slot]

        def accumulated(hf):
            return sum(k[0] == "Y" for k in flat[:flat.index(("B2", hf))])

        def max_bank(b, u):
            return 6 if b < 2 or u % 2 == 0 else 5

        N1T_OUT = 7
        KEYS_OUT = N1T_OUT + 8

        block = ctx.enter_context(nc.Block())

        @block.sync
        def _(sp):
            sp.dma_start(resid[:, :, :], x.rearrange(tiles, p=P)).then_inc(s_x, 16)
            w_view = w_qkv.rearrange("(hh p c) d -> p hh (c d)", p=P, c=3)
            sp.dma_start(b_nat[:, :, :], b_qkv.rearrange("(hh p c) -> p hh c", p=P, c=3)).then_inc(s_bias, 16)
            for i in range(4):
                sp.dma_start(w_in[:, 768 * i:768 * (i + 1)].rearrange("p (hh n) -> p hh n", hh=2),
                             w_view[:, 2 * i:2 * i + 2, :]).then_inc(s_w[i], 16)
            sp.dma_start(wo_nat, w_o).then_inc(s_wo, 16)
            sp.dma_start(ctx_nat, ctx_in.rearrange(tiles, p=P)).then_inc(s_ctx, 16)
            for i, w in enumerate((wq, wk, wv, wo)):
                sp.dma_start(wx[:, i, :], w).then_inc(s_wx, 16)
            with nc.allow_non_contiguous_dma(reason="128 biases, in the order of the permuted columns"):
                for i, v in enumerate((bq, bk)):
                    for par in range(2):
                        sp.dma_start(bqk[64 * par:64 * par + 64, i:i + 1],
                                      v[64 * par:64 * par + 64].rearrange("(g d) -> d g", d=DH)).then_inc(s_ffnb, 16)
            for i, v in enumerate((b_o, bv, bo)):
                sp.dma_start(brow[:, i, :], v.partition_broadcast(P)).then_inc(s_wx, 16)
            sp.dma_start(br_row[:, :], br.partition_broadcast(P)).then_inc(s_wx, 16)
            sp.dma_start(wr_sb[:, :], wr).then_inc(s_wx, 16)
            sp.dma_start(b1_nat[:, :], b1.rearrange("e (c p) -> (e c) p", p=P)).then_inc(s_ffnb, 16)
            sp.dma_start(b2_sb[:, :], b2).then_inc(s_ffnb, 16)
            sp.wait_ge(s_kpart, 3)
            sp.wait_ge(s_const, 5)
            for par in range(2):
                for n, part in enumerate(PARTS_K):
                    r = 64 * par + DH * n
                    sp.dma_start(k_st[r:r + DH, :, :], k_part[64 * par:64 * par + 64, part, :]).then_inc(s_kst, 16)

            def stack_q(b):
                sp.wait_ge(s_qpart, 3 * (b + 1))
                sp.wait_ge(s_qfree, b // 2 + 1)
                for par in range(2):
                    for n, part in enumerate(PARTS_Q):
                        r = 64 * par + DH * n
                        sp.dma_start(q_st[b][r:r + DH, :, S * par:S * par + S],
                                     q_part[64 * par:64 * par + 64, part, :]
                                     ).then_inc(s_qst[b], 16)

            def stack_m(b):
                sp.wait_ge(s_mpart, 3 * (b + 1))
                for par in range(2):
                    for part in range(3):
                        r = 64 * par + MAX_ROW + part
                        sp.dma_start(q_st[b][r:r + 1, :, S * par:S * par + S],
                                     m_part[8 * par:8 * par + 8, part, :]).then_inc(s_mst[b], 16)

            stack_q(0)
            stack_q(1)
            stack_m(0)
            stack_q(2)
            stack_m(1)
            stack_q(3)
            stack_m(2)
            sp.wait_ge(s_misc, misc_at[("PJ", B - 1)] + 1)
            sp.dma_start(w1_raw[:, :].rearrange("p (e n) -> p e n", n=HID), w1.rearrange("e p n -> p e n")
                         ).then_inc(s_w12[0], 16)
            sp.dma_start(w2_sb, w2.rearrange("e (c p) d -> p (e c) d", p=P)).then_inc(s_w12[1], 16)
            stack_m(3)
            for hf in range(2):
                sp.wait_ge(s_acc, NE * (hf + 1))
                sp.dma_start(out.rearrange(tiles, p=P)[:, 4 * hf:4 * hf + 4, :],
                             resid[:, 4 * hf:4 * hf + 4, :]).then_inc(s_out, 16)
            sp.wait_ge(s_out, 32)

        @block.gpsimd
        def _(pool):
            steps = [0]

            def step(ins):
                steps[0] += 1
                ins.then_inc(s_pool, 1)
                pool.wait_ge(s_pool, steps[0])

            step(pool.memset(ident[:, :], 0.0))
            pool.affine_select(out=ident[:, :], in_=ident[:, :], compare_op=ALU.not_equal, fill=1.0, base=0,
                               pattern=[[-1, P]], channel_multiplier=1).then_inc(s_const, 1)
            step(pool.memset(ident_b[:, :], 0.0))
            pool.affine_select(out=ident_b[:, :], in_=ident_b[:, :], compare_op=ALU.not_equal, fill=1.0, base=0,
                               pattern=[[-1, P]], channel_multiplier=1).then_inc(s_const, 1)
            pool.memset(one[:, :], 1.0)
            pool.memset(wk_mem[:, :], 0.0).then_inc(s_const, 1)
            step(pool.memset(mask[:, :, :], 0.0))
            pool.affine_select(out=mask[:, :, :], in_=mask[:, :, :], compare_op=ALU.is_ge, fill=MASKED, base=0,
                               pattern=[[0, 4], [1, P]], channel_multiplier=-1).then_inc(s_const, 1)
            step(pool.memset(half[:, :], -0.5))

            def rsqrt_of_var(n, t0, cnt):
                step(pool.tensor_scalar(tmp8[:, n, t0:t0 + cnt], mv[:, n, t0:t0 + cnt, 1], EPS_LN, None, ALU.add))
                step(pool.tensor_tensor(rstd[:, n, t0:t0 + cnt], tmp8[:, n, t0:t0 + cnt], half[:, 0:cnt], ALU.pow))
                step(pool.tensor_scalar(negm[:, n, t0:t0 + cnt], mv[:, n, t0:t0 + cnt, 0], -1.0, None, ALU.mult))

            pool.wait_ge(s_mv, NT)
            step(pool.tensor_scalar(tmp8[:, 0, :], mv[:, 0, :, 1], EPS_LN, EPS_RMS, ALU.add, ALU.mult))
            step(pool.tensor_tensor(tmp8[:, 0, :], tmp8[:, 0, :], mv[:, 0, :, 1], ALU.add))
            step(pool.tensor_scalar(negm[:, 0, :], mv[:, 0, :, 0], -1.0, None, ALU.mult))
            pool.tensor_tensor(rstd[:, 0, :], tmp8[:, 0, :], half[:, :], ALU.pow).then_inc(s_rstd, 1)

            def split(dst, src, rest, done):
                pool.tensor_copy(dst[0], src).then_inc(done, 1)
                pool.wait_ge(done, splits[done] + 1)
                step(pool.tensor_tensor(rest, src, dst[0], ALU.subtract))
                pool.tensor_copy(dst[1], rest).then_inc(done, 1)
                pool.wait_ge(done, splits[done] + 2)
                pool.tensor_tensor(dst[2], rest, dst[1], ALU.subtract).then_inc(done, 1)
                splits[done] += 3

            pool.memset(k_st[:, :, :].bitcast(F32), TWO_ONES).then_inc(s_const, 1)
            pool.memset(v_pad[:, :, :], 1.0).then_inc(s_const, 1)
            pool.iota(iota8[:, :], pattern=[[1, NE]], base=0, channel_multiplier=0,
                      allow_small_or_imprecise_dtypes=True).then_inc(s_const, 1)

            pool.wait_ge(s_wx, 144)
            pool.tensor_copy(wqk[:, :, :].rearrange("p i (r d g) -> p (i r) d g", r=2, d=DH),
                             wx[:, 0:2, :].rearrange("p i (r g d) -> p (i r) d g", r=2, d=DH)).then_inc(s_const, 1)
            splits = {s_kpart: 0, s_qpart: 0, s_mpart: 0}
            pool.wait_ge(s_n1, NT)
            pool.wait_ge(s_wx, 144)
            pool.tensor_tensor(resid[:, :, :], resid[:, :, :],
                               brow[:, 0:1, :].to_broadcast([P, NT, D]), ALU.add).then_inc(s_xb, 1)
            pool.wait_ge(s_set_ev, KEYS_OUT)
            split([k_part[:, i, :] for i in range(3)], k_f[:, :], k_r, s_kpart)
            pool.memset(q_mem0[:, :].bitcast(F32), 0.0).then_inc(s_qfree, 1)

            def norm_batch(n, b, s_in, s_norm):
                pool.wait_ge(s_in, TPB * (b + 1))
                rsqrt_of_var(n, TPB * b, TPB)
                for t in range(TPB * b, TPB * b + TPB):
                    pool.tensor_scalar(norm[:, t, :], resid[:, t, :], negm[:, n, t:t + 1], rstd[:, n, t:t + 1],
                                       ALU.add, ALU.mult).then_inc(s_norm, 1)

            def split_q(b):
                pool.wait_ge(s_misc_ev, misc_at[("q", b)] + 1)
                if b >= 1:
                    pool.wait_ge(s_qst[b - 1], 16 * 12)
                split([q_part[:, i, :] for i in range(3)], q_f[:, :], q_r[:, :], s_qpart)

            def split_m(b):
                pool.wait_ge(s_misc_ev, misc_at[("mT", b)] + 1)
                if b >= 1:
                    pool.wait_ge(s_mst[b - 1], 16 * 6)
                split([m_part[:, i, :] for i in range(3)], m_f[:, :], m_r[:, :], s_mpart)

            def norm_2(b):
                norm_batch(1, b, s_mv2, s_n2)
                pool.wait_ge(s_n2, TPB * (b + 1))
                pool.tensor_tensor(resid[:, TPB * b:TPB * b + TPB, :], resid[:, TPB * b:TPB * b + TPB, :],
                                   brow[:, 2:3, :].to_broadcast([P, TPB, D]), ALU.add).then_inc(s_xb2, 1)

            def norm_3(b):
                norm_batch(2, b, s_mv3, s_n3)

            norm_2(0)
            split_q(0)
            norm_2(1)
            split_q(1)
            split_m(0)
            norm_2(2)
            pool.wait_ge(s_t_lo, HP * B)
            pool.memset(q_mem1[:, :].bitcast(F32), 0.0).then_inc(s_qfree, 1)
            split_q(2)
            split_m(1)
            norm_2(3)
            split_q(3)
            split_m(2)
            norm_3(0)
            split_m(3)
            norm_3(1)
            norm_3(2)
            norm_3(3)
        @block.tensor
        def _(pe):
            pe.wait_ge(s_const, 4)
            for i in range(4):
                pe.wait_ge(s_wprep, 2 * i + 2)
                for hh in (2 * i, 2 * i + 1):
                    last = pe.matmul(ps[:, i, 256 * (hh % 2):256 * (hh % 2) + 256], w_nat[:, hh, 0, :],
                                     wk_blk[:, hh, :], start=True, stop=True)
                last.then_inc(s_set, 1)
            for t in range(NT):
                pe.wait_ge(s_n1, t + 1)
                last = pe.transpose(ps[:, 6 + t // 4, P * (t % 4):P * (t % 4) + P], norm[:, t, :], ident[:, :])
                if t % 4 == 3:
                    last.then_inc(s_set, 1)
            pe.wait_ge(s_wprep, 9)
            for h in range(H):
                last = pe.matmul(ps[:, 4, h:h + 1], wk_blk[:, h // 2, D * (h % 2):D * (h % 2) + D],
                                 b_q[:, h // 2:h // 2 + 1], start=True, stop=True)
            last.then_inc(s_set, 1)

            def products(out, a, b_):
                pe.matmul(out, a[0], b_[0], start=True, stop=False)
                pe.matmul(out, a[1], b_[0], start=False, stop=False)
                return pe.matmul(out, a[0], b_[1], start=False, stop=True)

            def ring_free(key):
                k = ring.index(key)
                if k >= 3:
                    kind, b, i = ring[k - 3]
                    if kind == "T":
                        pe.wait_ge(s_t_lo, HP * b + i + 1)
                    elif kind == "V":
                        pe.wait_ge(s_v_ev, 4 * b + i + 1)
                    else:
                        pe.wait_ge(s_z_ev, 4 * b + i + 1)
                return ps[:, ring_bank[key], :]

            def n_of(c0, n):
                return [n_parts[:, i, c0:c0 + n] for i in range(2)]

            def t_of(b, u):
                if b == 0:
                    pe.wait_ge(s_set_ev, N1T_OUT)
                    pe.wait_ge(s_set_lo, 6)
                bank = ring_free(("T", b, u))
                for h in (2 * u, 2 * u + 1):
                    last = products(bank[:, S * (h % 2):S * (h % 2) + S], [g[:, h, :] for g in G], n_of(S * b, S))
                last.then_inc(s_t, 1)

            def prepare(n):
                bank = 6 + n % 2
                if n == 0:
                    pe.wait_ge(s_wprep, 10)
                    pe.wait_ge(s_wo, 16)
                    pe.wait_ge(s_ctx, 16)
                if n >= 2:
                    pe.wait_ge(s_set_ev, N1T_OUT + n - 1)
                elif n == 1:
                    pe.wait_ge(s_set_ev, N1T_OUT)
                cols = ps[:, bank, :].rearrange("p (c n) -> p c n", n=P)
                if n == 2:
                    pe.wait_ge(s_set_lo, 7)
                if n == 3:
                    pe.wait_ge(s_set_lo, 8)
                if n == 6:
                    pe.wait_ge(s_wx, 144)
                    pe.wait_ge(s_const, 8)
                for c in range(4):
                    m = 4 * (n % 2) + c
                    if n < 2:
                        last = pe.transpose(cols[:, c, :], wv_c[:, m, :], ident[:, :])
                    elif n < 4:
                        last = pe.transpose(cols[:, c, :], wo_nat[:, P * m:P * m + P], ident[:, :])
                    elif n < 6:
                        last = pe.transpose(cols[:, c, :], ctx_nat[:, m, :], ident[:, :])
                    elif n < 8:
                        if c == 0:
                            last = pe.matmul(ps[:, bank, :], wqk[:, 1, :], ctxT[:, 512 * (n % 2):512 * (n % 2) + 512],
                                             start=True, stop=True)
                    else:
                        last = pe.matmul(cols[:, c, :], ctxT[:, P * m:P * m + P], wx[:, 2, :], start=True, stop=True)
                last.then_inc(s_set if n < 8 else s_vx, 1)

            def scores(b, s):
                k = 12 * b + s
                ge(pe, s_exp, k - 2)
                bank = ps[:, k % 3, :]
                if s % 3 < 2:
                    u = HP * b + 2 * (s // 3) + s % 3
                    pe.wait_ge(s_t_lo, u + 1)
                    for a, t in ((0, 0), (1, 0), (0, 1)):
                        pe.matmul(bank, n_parts[:, a, S * b:S * b + P], t_ring[t][:, 2 * (u % 6):2 * (u % 6) + 2, :],
                                  start=(a + t == 0), stop=False)
                    pe.matmul(bank.rearrange("p (h q) -> p h q", h=2)[:, :, 0:P], ident_b[:, :], mask[:, 0:2, :],
                              start=False, stop=True).then_inc(s_sc, 1)
                else:
                    u = HP * b + 2 * (s // 3)
                    for a, t in ((0, 0), (1, 0), (0, 1)):
                        pe.matmul(bank, n_parts[:, a, S * b + P:S * b + S], t_ring[t][:, 2 * (u % 6):2 * (u % 6) + 4, P:S],
                                  start=(a + t == 0), stop=False)
                    pe.matmul(bank, ident_b[:, :], mask[:, :, :], start=False, stop=True).then_inc(s_sc, 1)

            def values(b, i):
                if b == 0 and i == 0:
                    pe.wait_ge(s_set_ev, N1T_OUT + 2)
                    pe.wait_ge(s_set_lo, 8)
                bank = ring_free(("V", b, i))
                kt, hf = i % 2, i // 2
                products(bank, n_of(S * b + P * kt, P), [wvT[:, j, 512 * hf:512 * hf + 512] for j in range(2)]
                         ).then_inc(s_v, 1)

            def heads_out(b, zu):
                bank = ring_free(("Z", b, zu))
                pe.wait_ge(s_exp, 12 * b + 3 * zu + 3)
                pe.wait_ge(s_v_ev, 4 * b + 2 * (zu // 2) + 2)
                for pair in (2 * zu, 2 * zu + 1):
                    c0 = S * (pair % 2)
                    for kt in range(2):
                        for hp in range(2):
                            h = 2 * pair + hp
                            v = v_sb[:, kt, E1 * h:E1 * h + E1]
                            o = bank[64 * hp:64 * hp + 64, c0:c0 + S]
                            if kt == 0:
                                last = pe.matmul(o, v, p0[:, h, :], start=True, stop=False)
                            else:
                                last = pe.matmul(o[:, P:S], v, p1[:, h, :], start=False, stop=True)
                last.then_inc(s_z, 1)

            def project(b):
                if b == 0:
                    pe.wait_ge(s_set_ev, N1T_OUT + 4)
                misc(("PJ", b))
                pe.wait_ge(s_z_ev, 4 * b + 4)
                for i in range(TPB):
                    for c in range(HP):
                        last = pe.matmul(ps[:, 7, P * i:P * i + P], zT[:, c, P * i:P * i + P], woT[:, c, :],
                                         start=(c == 0), stop=(c == HP - 1))
                last.then_inc(s_misc, 1)

            def misc(key):
                if misc_at[key] == 0:
                    pe.wait_ge(s_vx_ev, 2)
                ge(pe, s_misc_ev, misc_at[key])

            def query(b, n):
                if n == 0:
                    misc(("n2T", b))
                    pe.wait_ge(s_n2, TPB * (b + 1))
                    for i in range(TPB):
                        last = pe.transpose(ps[:, 7, P * i:P * i + P], norm[:, TPB * b + i, :], ident[:, :])
                else:
                    misc(("q", b))
                    last = pe.matmul(ps[:, 7, 0:S], wqk[:, 0, :], n2T[:, :], start=True, stop=True)
                last.then_inc(s_misc, 1)

            def max_scores(b, u):
                g, qt = u // 2, u % 2
                if u == 0:
                    pe.wait_ge(s_qst[b], 16 * 12)
                    if b == 0:
                        pe.wait_ge(s_kst, 16 * 12)
                        pe.wait_ge(s_vx_ev, 1)
                    if b == 2:
                        pe.wait_ge(s_z_ev, 4 * B)
                ge(pe, s_mx_ev, 16 * b + u - (1 if b >= 2 and (b, u) != (2, 0) else 0))
                for par in range(2):
                    last = pe.matmul(ps[:, max_bank(b, u), S * par:S * par + S],
                                     q_st[b][:, g, S * par + P * qt:S * par + P * qt + P],
                                     k_st[:, g, S * b:S * b + S], start=True, stop=True)
                last.then_inc(s_mx, 1)

            def max_turn(b):
                misc(("mT", b))
                pe.wait_ge(s_mx_ev, 16 * b + 16)
                for i in range(TPB):
                    last = pe.transpose(ps[0:H, 7, P * i:P * i + P], mneg[:, i, :], ident[:, :])
                last.then_inc(s_misc, 1)

            def cross_scores(b, g):
                if g == 0:
                    pe.wait_ge(s_mst[b], 16 * 6)
                for kt in range(2):
                    k = 2 * (HP * b + g) + kt
                    if k < 3:
                        pe.wait_ge(s_exp, 12 * B - 2 + k)
                    else:
                        pe.wait_ge(s_px, k - 2)
                    pe.matmul(ps[:, k % 3, :], k_st[:, g, S * b + P * kt:S * b + P * kt + P], q_st[b][:, g, :],
                              start=True, stop=True).then_inc(s_st, 1)

            def cross_out(b, g4):
                pe.wait_ge(s_px, 16 * b + 4 * g4 + 4)
                m = 2 * b + g4 // 2
                if m < 2:
                    pe.wait_ge(s_z_ev, 4 * B)
                else:
                    pe.wait_ge(s_pv_ev, m - 1)
                for kt in range(2):
                    for j in range(4):
                        h = 2 * g4 + j // 2 + 8 * (j % 2)
                        p = px[:, g4 % 2, 1024 * (j // 2) + 512 * kt + S * (j % 2):][:, 0:S]
                        last = pe.matmul(ps[32 * j:32 * j + 32, 3 + m % 2, S * (g4 % 2):S * (g4 % 2) + S],
                                         v_pad[:, TPB * b + kt, (DH + 1) * h:(DH + 1) * h + 32], p, start=(kt == 0), stop=(kt == 1))
                last.then_inc(s_pv, 1)

            def out_step(b, n):
                if n in (0, 2):
                    qt = n // 2
                    misc((f"oq{qt}", b))
                    pe.wait_ge(s_pv_ev, 2 * b + 2)
                    for g4 in range(4):
                        last = pe.transpose(ps[:, 7, P * g4:P * g4 + P], o_raw[:, g4, P * qt:P * qt + P], ident[:, :])
                elif n in (1, 3):
                    qt = n // 2
                    misc((f"oT{qt}", b))
                    last = pe.transpose(ps[:, 7, 0:P], o_n[:, qt, :], ident[:, :])
                else:
                    misc(("wo", b))
                    for i in range(TPB):
                        last = pe.matmul(ps[:, 7, P * i:P * i + P], oT[:, P * i:P * i + P], wx[:, 3, :],
                                         start=True, stop=True)
                last.then_inc(s_misc, 1)

            def expert_step(kind, hf):
                misc((kind, hf))
                ts = range(4 * hf, 4 * hf + 4)
                if kind == "b1":
                    pe.wait_ge(s_ffnb, 96)
                    last = pe.transpose(ps[:, 7, 0:NE * NC], b1_nat[:, :], ident[0:NE * NC, 0:NE * NC])
                elif kind == "NT":
                    pe.wait_ge(s_n3, 4 * hf + 4)
                    for t in ts:
                        last = pe.transpose(ps[:, 7, P * (t % 4):P * (t % 4) + P], norm[:, t, :], ident[:, :])
                elif kind == "RT":
                    for t in ts:
                        for i in range(2):
                            last = pe.matmul(ps[:, 7, NE * (t % 4):NE * (t % 4) + NE],
                                             n_parts[:, i, P * t:P * t + P].bitcast(F32), wr_sb[:, :],
                                             start=(i == 0), stop=(i == 1))
                elif kind == "WT":
                    pe.wait_ge(s_wgt, hf + 1)
                    for t in ts:
                        last = pe.transpose(ps[0:NE, 7, P * (t % 4):P * (t % 4) + P], wgt[:, t, :], ident[:, :])
                else:
                    for t in ts:
                        last = pe.matmul(ps[:, 7, P * (t % 4):P * (t % 4) + P], wgtT[:, P * t:P * t + P],
                                         b2_sb[:, :], start=True, stop=True)
                last.then_inc(s_misc, 1)

            def hidden(k, c):
                e, hf = k % NE, k // NE
                if k == 0 and c == 0:
                    pe.wait_ge(s_wlo, 8)
                    pe.wait_ge(s_px, 16 * B)
                    pe.wait_ge(s_mx_ev, 16 * B)
                if k % NE == 0 and c == 0:
                    pe.wait_ge(s_misc_ev, misc_at[("NT", hf)] + 1)
                if k >= 1:
                    pe.wait_ge(s_ha if c % 2 == 0 else s_hd, 2 * (k - 1) + c // 2 + 1)
                products(ps[:, H_BANK[c], :], [w[:, e, P * c:P * c + P] for w in w1_p], n_of(512 * hf, 512)).then_inc(s_h, 1)

            def combine(k):
                e = k % NE
                if k == 0:
                    pe.wait_ge(s_w12[1], 16)
                    pe.wait_ge(s_pv_ev, 2 * B)
                ge(pe, s_acc, k - 1)
                pe.wait_ge(s_ha, 2 * k + 2)
                pe.wait_ge(s_hd, 2 * k + 2)
                for tt in range(4):
                    for c in range(NC):
                        last = pe.matmul(ps[:, Y_BANK[k % 2], P * tt:P * tt + P], hid[:, k % 2, c, P * tt:P * tt + P],
                                         w2_sb[:, NC * e + c, :], start=(c == 0), stop=(c == NC - 1))
                last.then_inc(s_y, 1)

            for slot in slots:
                for kind, b, *i in slot:
                    if kind == "S":
                        scores(b, *i)
                    elif kind == "T":
                        t_of(b, *i)
                    elif kind == "V":
                        values(b, *i)
                    elif kind == "Z":
                        heads_out(b, *i)
                    elif kind == "P":
                        prepare(*i)
                    elif kind == "PJ":
                        project(b)
                    elif kind in ("n2T", "q"):
                        query(b, kind == "q")
                    elif kind == "MX":
                        max_scores(b, *i)
                    elif kind == "mT":
                        max_turn(b)
                    elif kind == "CS":
                        cross_scores(b, *i)
                    elif kind == "CO":
                        cross_out(b, *i)
                    elif kind in ("oq0", "oT0", "oq1", "oT1", "wo"):
                        out_step(b, ("oq0", "oT0", "oq1", "oT1", "wo").index(kind))
                    elif kind == "H":
                        hidden(b, *i)
                    elif kind == "Y":
                        combine(b)
                    elif kind in ("b1", "NT", "RT", "WT", "B2"):
                        expert_step(kind, b)


        @block.scalar
        def _(act):
            def copy_out(n, dst, src):
                act.wait_ge(s_set, n + 1)
                act.copy(dst, src).then_inc(s_set_ev, 1)

            for i in range(4):
                copy_out(i, G[0][:, 4 * i:4 * i + 4, :], ps[:, i, :])
            act.wait_ge(s_const, 3)
            for i in range(2):
                act.wait_ge(s_set, 5 + i)
                act.activation(n_parts[:, 0, 512 * i:512 * i + 512], ps[:, 6 + i, :], ACT.Identity, bias=one[:, 0:1]
                               ).then_inc(s_set_ev, 1)
            copy_out(6, cvec[:, :], ps[:, 4, 0:H])

            def prepared(n):
                i = n % 2
                cols = slice(512 * i, 512 * i + 512)
                if n < 6:
                    dst = (wvT[:, 0, cols], woT[:, 4 * i:4 * i + 4, :], ctxT[:, cols])[n // 2]
                    copy_out(N1T_OUT + n, dst, ps[:, 6 + i, :])
                elif n < 8:
                    if n == 6:
                        act.wait_ge(s_ffnb, 96)
                    act.wait_ge(s_set, N1T_OUT + n + 1)
                    act.activation(k_f[:, cols], ps[:, 6 + i, :], ACT.Identity, bias=bqk[:, 1:2]).then_inc(s_set_ev, 1)

            def t_high(b, u):
                k = HP * b + u
                act.wait_ge(s_t, k + 1)
                if k >= 6:
                    last_use = k - 6
                    act.wait_ge(s_sc, 12 * (last_use // HP) + 3 * (last_use % HP // 2) + 3)
                bank = ps[:, ring_bank[("T", b, u)], :]
                for i in range(2):
                    last = act.activation(t_ring[0][:, 2 * (k % 6) + i, :], bank[:, S * i:S * i + S], ACT.Identity,
                                          bias=cvec[:, 2 * u + i:2 * u + i + 1])
                last.then_inc(s_t_hi, 1)

            def probabilities(b, u):
                k = 12 * b + u
                act.wait_ge(s_max, k + 1)
                bank = ps[:, k % 3, :]
                j = u // 3
                if u % 3 < 2:
                    heads, kt, n = range(4 * j + 2 * (u % 3), 4 * j + 2 * (u % 3) + 2), 0, S
                else:
                    heads, kt, n = range(4 * j, 4 * j + 4), 1, P
                for i, h in enumerate(heads):
                    dst = p0[:, h, :] if kt == 0 else p1[:, h, :]
                    last = act.activation(dst, bank[:, n * i:n * i + n], ACT.Exp, bias=negmax[:, kt, h:h + 1],
                                          accum_out=psums[:, kt, h:h + 1])
                last.then_inc(s_exp, 1)

            def query_out(b, n):
                if n == 0:
                    act.wait_ge(s_misc, misc_at[("n2T", b)] + 1)
                    act.copy(n2T[:, :], ps[:, 7, 0:S]).then_inc(s_misc_ev, 1)
                    return
                act.wait_ge(s_misc, misc_at[("q", b)] + 1)
                ge(act, s_qpart, 3 * b)
                act.activation(q_f[:, :], ps[:, 7, 0:S], ACT.Identity, bias=bqk[:, 0:1]).then_inc(s_misc_ev, 1)

            def max_out(b):
                act.wait_ge(s_misc, misc_at[("mT", b)] + 1)
                ge(act, s_mpart, 3 * b)
                act.copy(m_f[:, :], ps[0:H, 7, 0:S]).then_inc(s_misc_ev, 1)

            def z_out(b, i):
                act.wait_ge(s_z, 4 * b + i + 1)
                if b >= 1:
                    act.wait_ge(s_misc, misc_at[("PJ", b - 1)] + 1)
                act.copy(zT[:, 2 * i:2 * i + 2, :], ps[:, ring_bank[("Z", b, i)], :]).then_inc(s_z_ev, 1)

            def cross_probabilities(b, g):
                for kt in range(2):
                    k = 2 * (HP * b + g) + kt
                    act.wait_ge(s_st, k + 1)
                    ge(act, s_pv, 4 * b + g // 2 - 1)
                    c0 = 1024 * (g % 2) + 512 * kt
                    act.activation(px[:, (g // 2) % 2, c0:c0 + 512], ps[:, k % 3, :], ACT.Exp,
                                   scale=SCALE_X).then_inc(s_px, 1)

            def cross_copy(b, i):
                act.wait_ge(s_pv, 4 * b + 2 * i + 2)
                if b == 0 and i == 0:
                    act.wait_ge(s_kpart, 3)
                if i == 0:
                    ge(act, s_misc, misc_at[("oq1", b - 1)] + 1 if b else 0)
                act.copy(o_raw[:, 2 * i:2 * i + 2, :], ps[:, 3 + i, :]).then_inc(s_pv_ev, 1)

            def out_copy(b, qt):
                act.wait_ge(s_misc, misc_at[(f"oT{qt}", b)] + 1)
                act.copy(oT[:, P * qt:P * qt + P], ps[:, 7, 0:P]).then_inc(s_misc_ev, 1)

            def weight_high(i):
                act.wait_ge(s_w12[0], 16)
                act.copy(w1_hi[:, 512 * i:512 * i + 512], w1_raw[:, 512 * i:512 * i + 512]).then_inc(s_whi, 1)

            def relu(k, c):
                act.wait_ge(s_h, 4 * k + c + 1)
                ge(act, s_y, k - 1)
                act.activation(hid[:, k % 2, c, :], ps[:, H_BANK[c], :], ACT.Relu,
                               bias=b1T[:, NC * (k % NE) + c:NC * (k % NE) + c + 1]).then_inc(s_ha, 1)

            def expert_copy(kind, hf):
                cols = slice(512 * hf, 512 * hf + 512)
                if kind == "RT":
                    act.wait_ge(s_score, 2 * hf + 2)
                    act.activation(gate[:, 1, 4 * hf:4 * hf + 4], gate[:, 0, 4 * hf:4 * hf + 4], ACT.Exp).then_inc(s_ed, 1)
                    return
                act.wait_ge(s_misc, misc_at[(kind, hf)] + 1)
                if kind == "b1":
                    act.copy(b1T[:, :], ps[:, 7, 0:NE * NC]).then_inc(s_misc_ev, 1)
                elif kind == "NT":
                    act.copy(n_parts[:, 0, cols], ps[:, 7, :]).then_inc(s_n3T, 1)
                else:
                    act.copy(wgtT[:, cols], ps[0:NE, 7, :]).then_inc(s_misc_ev, 1)

            for slot in slots:
                for kind, b, *i in slot:
                    if kind == "T":
                        t_high(b, *i)
                for kind, b, *i in slot:
                    if kind == "S":
                        probabilities(b, *i)
                    elif kind == "Z":
                        z_out(b, *i)
                    elif kind == "P" and i[0] < 8:
                        prepared(*i)
                    elif kind in ("n2T", "q"):
                        query_out(b, kind == "q")
                    elif kind == "mT":
                        max_out(b)
                    elif kind == "CS":
                        cross_probabilities(b, *i)
                    elif kind == "CO" and i[0] % 2 == 1:
                        cross_copy(b, i[0] // 2)
                    elif kind in ("oT0", "oT1"):
                        out_copy(b, int(kind == "oT1"))
                    elif kind == "WS":
                        weight_high(*i)
                    elif kind == "H" and i[0] % 2 == 0:
                        relu(b, *i)
                    elif kind in ("b1", "NT", "RT", "WT"):
                        expert_copy(kind, b)

        @block.vector
        def _(dve):
            steps = [0]

            def step(ins):
                steps[0] += 1
                ins.then_inc(s_dve, 1)
                dve.wait_ge(s_dve, steps[0])

            dve.wait_ge(s_x, 16)
            for t in range(NT):
                dve.bn_stats(stats[:, t, :], resid[:, t, :]).then_inc(s_bn, 1)
            dve.wait_ge(s_bn, NT)
            for t in range(NT):
                dve.bn_aggr(mv[:, 0, t, :], stats[:, t, :]).then_inc(s_mv, 1)

            def first_norm():
                dve.wait_ge(s_rstd, 1)
                for t in range(NT):
                    dve.tensor_scalar(norm[:, t, :], resid[:, t, :], negm[:, 0, t:t + 1], rstd[:, 0, t:t + 1],
                                      ALU.add, ALU.mult).then_inc(s_n1, 1)

            dve.wait_ge(s_bias, 16)
            step(dve.tensor_scalar(b_over_d[:, :, :], b_nat[:, :, 1:3], 1.0 / D, None, ALU.mult))
            dve.wait_ge(s_const, 3)

            def row_addition(c, hs):
                step(dve.tensor_reduce(row_add[:, c, hs], w_nat[:, hs, 1 + c, :], AX, ALU.add))
                step(dve.scalar_tensor_tensor(row_add[:, c, hs], row_add[:, c, hs], -1.0 / D, b_over_d[:, hs, c],
                                              ALU.mult, ALU.add))

            for i in range(4):
                dve.wait_ge(s_w[i], 16)
                hs = slice(2 * i, 2 * i + 2)
                step(dve.tensor_reduce(b_q[:, hs], w_nat[:, hs, 0, :], AX, ALU.add))
                row_addition(0, hs)
                for hp in range(2):
                    r = slice(64 * hp, 64 * hp + 64)
                    dve.tensor_tensor(wk_blk[r, hs, D * hp:D * hp + D], w_nat[r, hs, 1, :],
                                      row_add[r, 0, hs].unsqueeze(2).to_broadcast([64, 2, D]), ALU.add
                                      ).then_inc(s_wprep, 1)
                if i == 1:
                    first_norm()
            dve.tensor_tensor(b_q[:, :], b_nat[:, :, 0], b_q[:, :], ALU.subtract).then_inc(s_wprep, 1)
            row_addition(1, slice(0, HP))
            dve.tensor_tensor(wv_c, w_nat[:, :, 2, :], row_add[:, 1, :].unsqueeze(2).to_broadcast([P, HP, D]),
                              ALU.add).then_inc(s_wprep, 1)

            def low(dst, src, const, high, s_done):
                dve.scalar_tensor_tensor(dst, src, const, high.bitcast(F32), ALU.add, ALU.subtract).then_inc(s_done, 1)

            for i in range(4):
                dve.wait_ge(s_set_ev, i + 1)
                low(G[1][:, 4 * i:4 * i + 4, :], ps[:, i, :].rearrange("p (h n) -> p h n", n=D), 0.0,
                    G[0][:, 4 * i:4 * i + 4, :], s_set_lo)
            for i in range(2):
                dve.wait_ge(s_set_ev, 5 + i)
                cols = slice(512 * i, 512 * i + 512)
                low(n_parts[:, 1, cols], ps[:, 6 + i, :], 1.0, n_parts[:, 0, cols], s_set_lo)

            def prepare_low(n):
                dve.wait_ge(s_set_ev, N1T_OUT + n + 1)
                low(wvT[:, 1, 512 * n:512 * n + 512], ps[:, 6 + n, :], 0.0, wvT[:, 0, 512 * n:512 * n + 512], s_set_lo)

            def t_low(b, u):
                k = HP * b + u
                dve.wait_ge(s_t_hi, k + 1)
                bank = ps[:, ring_bank[("T", b, u)], :]
                for i in range(2):
                    h = 2 * (k % 6) + i
                    last = dve.scalar_tensor_tensor(t_ring[1][:, h, :], bank[:, S * i:S * i + S],
                                                    cvec[:, 2 * u + i:2 * u + i + 1], t_ring[0][:, h, :].bitcast(F32),
                                                    ALU.add, ALU.subtract)
                last.then_inc(s_t_lo, 1)

            def cross_values(i):
                dve.wait_ge(s_vx, i + 1)
                dve.wait_ge(s_wx, 144)
                dve.wait_ge(s_const, 6)
                dve.tensor_tensor(v_heads[:, 4 * i:4 * i + 4, :, 0:DH],
                                  ps[:, 6 + i, :].rearrange("p (t h d) -> p t h d", t=4, h=H),
                                  brow[:, 1, :].rearrange("p (h d) -> p h d", d=DH).unsqueeze(1).to_broadcast([P, 4, H, DH]),
                                  ALU.add).then_inc(s_vx_ev, 1)

            def maxima(b, u):
                k = 12 * b + u
                dve.wait_ge(s_sc, k + 1)
                j = u // 3
                if u % 3 < 2:
                    dst, n = negmax[:, 0, 4 * j + 2 * (u % 3):4 * j + 2 * (u % 3) + 2], 2
                else:
                    dst, n = negmax[:, 1, 4 * j:4 * j + 4], 4
                dve.tensor_reduce(dst, ps[:, k % 3, :].rearrange("p (h q) -> p h q", h=n), AX, ALU.max,
                                  negate=True).then_inc(s_max, 1)

            def values_out(b, u):
                kt, hf = u % 2, u // 2
                dve.wait_ge(s_exp, 12 * b + 6 * hf + 6)
                hs = slice(8 * hf, 8 * hf + 8)
                step(dve.reciprocal(rsum[:, kt, hs], psums[:, kt, hs]))
                dve.wait_ge(s_v, 4 * b + u + 1)
                if b >= 1:
                    dve.wait_ge(s_z, 4 * (b - 1) + 2 * hf + 2)
                dve.tensor_tensor(v_sb[:, kt, 512 * hf:512 * hf + 512].rearrange("p (h e) -> p h e", e=E1),
                                  ps[:, ring_bank[("V", b, u)], :].rearrange("p (h e) -> p h e", e=E1),
                                  rsum[:, kt, hs].unsqueeze(2).to_broadcast([P, 8, E1]), ALU.mult).then_inc(s_v_ev, 1)

            def residual(n, b, s_done, count, s_stat):
                ts = slice(TPB * b, TPB * b + TPB)
                dve.tensor_tensor(resid[:, ts, :], ps[:, 7, 0:S].rearrange("p (t d) -> p t d", d=D),
                                  resid[:, ts, :], ALU.add).then_inc(s_done, 1)
                dve.wait_ge(s_done, count)
                for t in range(TPB * b, TPB * b + TPB):
                    step(dve.bn_stats(stats[:, t, :], resid[:, t, :]))
                    dve.bn_aggr(mv[:, n, t, :], stats[:, t, :]).then_inc(s_stat, 1)

            def cross_max(b, u):
                g, qt = u // 2, u % 2
                dve.wait_ge(s_mx, 16 * b + u + 1)
                if u == 0 and b >= 1:
                    dve.wait_ge(s_misc, misc_at[("mT", b - 1)] + 1)
                dve.tensor_reduce(mneg[:, qt, :].rearrange("p (r g) -> p r g", r=2)[:, :, g],
                                  ps[:, max_bank(b, u), :].rearrange("p (h k) -> p h k", h=2), AX, ALU.max,
                                  negate=True).then_inc(s_mx_ev, 1)

            def self_residual(b):
                dve.wait_ge(s_misc, misc_at[("PJ", b)] + 1)
                dve.wait_ge(s_xb, 1)
                residual(1, b, s_misc_ev, misc_at[("PJ", b)] + 1, s_mv2)

            def cross_normalise(b, qt):
                dve.wait_ge(s_misc, misc_at[(f"oq{qt}", b)] + 1)
                turned = ps[:, 7, :].rearrange("p (g j r) -> p g j r", g=4, j=4)
                step(dve.reciprocal(r_den[:, qt, :].rearrange("p (g j) -> p g j", g=4), turned[:, :, :, DH]))
                for par in range(2):
                    src = turned[:, :, :, :].rearrange("p g (a r) c -> p g a r c", r=2)[:, :, :, par, 0:DH]
                    den = r_den[:, qt, :].rearrange("p (g a r) -> p g a r", g=4, r=2)[:, :, :, par]
                    last = (dve.tensor_tensor(o_n[:, qt, 64 * par:64 * par + 64].rearrange("p (g a d) -> p g a d", g=4, d=DH),
                                           src, den.unsqueeze(3).to_broadcast([P, 4, 2, DH]), ALU.mult))
                last.then_inc(s_misc_ev, 1)

            def cross_residual(b):
                dve.wait_ge(s_misc, misc_at[("wo", b)] + 1)
                dve.wait_ge(s_xb2, b + 1)
                residual(2, b, s_misc_ev, misc_at[("wo", b)] + 1, s_mv3)

            def weight_low(i):
                dve.wait_ge(s_whi, i + 1)
                cols = slice(512 * i, 512 * i + 512)
                dve.tensor_tensor(w1_lo[:, cols], w1_raw[:, cols], w1_hi[:, cols].bitcast(F32), ALU.subtract
                                  ).then_inc(s_wlo, 1)

            def norm_low(hf):
                dve.wait_ge(s_n3T, hf + 1)
                cols = slice(512 * hf, 512 * hf + 512)
                low(n_parts[:, 1, cols], ps[:, 7, :], 0.0, n_parts[:, 0, cols], s_misc_ev)

            def best_two(hf):
                ts = slice(4 * hf, 4 * hf + 4)
                dve.wait_ge(s_misc, misc_at[("RT", hf)] + 1)
                step(dve.tensor_copy(score[:, ts, :], ps[:, 7, 0:4 * NE].rearrange("p (t e) -> p t e", e=NE)))
                dve.tensor_tensor(score[:, ts, :], score[:, ts, :], br_row[:, :].unsqueeze(1).to_broadcast([P, 4, NE]),
                                  ALU.add).then_inc(s_misc_ev, 1)
                dve.wait_ge(s_misc_ev, misc_at[("RT", hf)] + 1)
                for t in range(4 * hf, 4 * hf + 4):
                    step(dve.max(top[:, t, :], score[:, t, :]))
                    last = dve.max_index(top_i[:, t, :], top[:, t, :], score[:, t, :])
                last.then_inc(s_score, 1)
                dve.wait_ge(s_score, 2 * hf + 1)
                dve.tensor_tensor(gate[:, 0, ts], top[:, ts, 1], top[:, ts, 0], ALU.subtract).then_inc(s_score, 1)

            def gates(hf):
                ts = slice(4 * hf, 4 * hf + 4)
                step(dve.tensor_copy(top_f[:, ts, :], top_i[:, ts, 0:2]))
                for n in range(2):
                    step(dve.tensor_tensor(hot[:, n, ts, :], iota8[:, :].unsqueeze(1).to_broadcast([P, 4, NE]),
                                           top_f[:, ts, n:n + 1].to_broadcast([P, 4, NE]), ALU.is_equal))
                dve.wait_ge(s_ed, hf + 1)
                step(dve.tensor_scalar(gate[:, 2, ts], gate[:, 1, ts], 1.0, None, ALU.add))
                step(dve.reciprocal(gate[:, 2, ts], gate[:, 2, ts]))
                step(dve.tensor_tensor(gate[:, 3, ts], gate[:, 1, ts], gate[:, 2, ts], ALU.mult))
                for n in range(2):
                    step(dve.tensor_tensor(hot[:, n, ts, :], hot[:, n, ts, :],
                                           gate[:, 2 + n, ts].unsqueeze(2).to_broadcast([P, 4, NE]), ALU.mult))
                dve.tensor_tensor(wgt[:, ts, :], hot[:, 0, ts, :], hot[:, 1, ts, :], ALU.add).then_inc(s_wgt, 1)
                dve.wait_ge(s_wgt, hf + 1)

            def relu(k, c):
                dve.wait_ge(s_h, 4 * k + c + 1)
                ge(dve, s_y, k - 1)
                dve.tensor_scalar(hid[:, k % 2, c, :], ps[:, H_BANK[c], :], b1T[:, NC * (k % NE) + c:NC * (k % NE) + c + 1],
                                  0.0, ALU.add, ALU.max).then_inc(s_hd, 1)

            def bias_sum(hf):
                ts = slice(4 * hf, 4 * hf + 4)
                dve.wait_ge(s_misc, misc_at[("B2", hf)] + 1)
                dve.wait_ge(s_n3, 4 * hf + 4)
                ge(dve, s_acc, accumulated(hf))
                dve.tensor_tensor(resid[:, ts, :], ps[:, 7, :].rearrange("p (t d) -> p t d", d=D),
                                  resid[:, ts, :], ALU.add).then_inc(s_misc_ev, 1)
                dve.wait_ge(s_misc_ev, misc_at[("B2", hf)] + 1)

            def accumulate(k):
                e, hf = k % NE, k // NE
                dve.wait_ge(s_y, k + 1)
                dve.wait_ge(s_n3, 4 * hf + 4)
                ge(dve, s_acc, k)
                for tt in range(4):
                    t = 4 * hf + tt
                    last = dve.scalar_tensor_tensor(resid[:, t, :], ps[:, Y_BANK[k % 2], P * tt:P * tt + P],
                                                    wgt[:, t, e:e + 1], resid[:, t, :], ALU.mult, ALU.add)
                last.then_inc(s_acc, 1)

            for slot in slots:
                for kind, b, *i in slot:
                    if kind == "S":
                        maxima(b, *i)
                    elif kind == "T":
                        t_low(b, *i)
                    elif kind == "V":
                        values_out(b, *i)
                    elif kind == "P" and i[0] < 2:
                        prepare_low(*i)
                    elif kind == "P" and i[0] >= 8:
                        cross_values(i[0] - 8)
                    elif kind == "PJ":
                        self_residual(b)
                    elif kind == "MX":
                        cross_max(b, *i)
                    elif kind in ("oq0", "oq1"):
                        cross_normalise(b, int(kind == "oq1"))
                    elif kind == "wo":
                        cross_residual(b)
                    elif kind == "WS":
                        weight_low(*i)
                    elif kind == "NT":
                        norm_low(b)
                    elif kind == "RT":
                        best_two(b)
                    elif kind == "GT":
                        gates(b)
                    elif kind == "B2":
                        bias_sum(b)
                    elif kind == "H" and i[0] % 2 == 1:
                        relu(b, *i)
                    elif kind == "Y":
                        accumulate(b)


_INS = ['x', 'ctx_1024', 'L0_attn_W_qkv', 'L0_attn_b_qkv', 'L0_attn_W_o', 'L0_attn_b_o',
        'L0_xattn_Wq', 'L0_xattn_bq', 'L0_xattn_Wk', 'L0_xattn_bk', 'L0_xattn_Wv', 'L0_xattn_bv',
        'L0_xattn_Wo', 'L0_xattn_bo', 'L0_ffn_Wr', 'L0_ffn_br', 'L0_ffn_W1', 'L0_ffn_b1', 'L0_ffn_W2', 'L0_ffn_b2']


def kernel(**inputs):
    import numpy as _np
    import concourse.bacc as _bacc
    from concourse import mybir as _mybir
    from concourse.bass_utils import run_bass_kernel_spmd as _run

    nc = _bacc.Bacc("TRN2", target_bir_lowering=False, num_devices=1)
    arrays, args = {}, []
    for name in _INS:
        a = _np.ascontiguousarray(inputs[name])
        arrays[f"in_{name}"] = a
        args.append(nc.dram_tensor(f"in_{name}", a.shape, _mybir.dt.from_np(a.dtype), kind="ExternalInput").ap())
    shape = arrays["in_x"].shape
    args.append(nc.dram_tensor("out_dram", shape, _mybir.dt.float32, kind="ExternalOutput").ap())
    decoder_layer(nc, *args)
    r = _run(nc, [arrays], core_ids=[0])
    return r.results[0]["out_dram"]
```

```python
from contextlib import ExitStack

import concourse.bass as bass
from concourse import mybir

F32 = mybir.dt.float32
F32R = mybir.dt.float32r
BF16 = mybir.dt.bfloat16
U32 = mybir.dt.uint32
ALU = mybir.AluOpType
ACT = mybir.ActivationFunctionType
AX = mybir.AxisListType.X

P = 128
B, S, D = 4, 256, 128
NT = B * S // P
TPB = S // P
H, E1 = 16, 64
HP = H // 2
DH = 8
NE, HID = 8, 512
NC = HID // P
EPS_LN, EPS_RMS = 1e-5, 1.1920929e-07
MASKED = -1.0e38
WARM_UP = 13
PARTS_Q = (0, 0, 0, 1, 1, 2)
PARTS_K = (0, 1, 2, 0, 1, 0)
MAX_ROW = DH * len(PARTS_Q)
TWO_ONES = 1.0 + 0x3F80 / 2.0 ** 23
SCALE_X = float(DH) ** -0.5


def ge(eng, sem, value):
    if value > 0:
        eng.wait_ge(sem, value)


def decoder_layer(nc, x, ctx_in, w_qkv, b_qkv, w_o, b_o, wq, bq, wk, bk, wv, bv, wo, bo,
                  wr, br, w1, b1, w2, b2, out):
    ctx = ExitStack()
    with ctx:
        def sb(name, shape, dt=F32):
            return ctx.enter_context(nc.sbuf_tensor(name, shape, dt))

        def sem(name):
            return ctx.enter_context(nc.semaphore(name))

        resid = sb("resid", [P, NT, D])

        def overlay(*layouts):
            made = []
            for n, layout in enumerate(layouts):
                kept = ctx if n == len(layouts) - 1 else ExitStack()
                made += [kept.enter_context(nc.sbuf_tensor(name, [P, cols], dt)) for name, cols, dt in layout]
                if kept is not ctx:
                    kept.close()
            return made

        w_in, q_mem0, hid = overlay([("w_in", 4096, F32)], [("q_mem0", 8192, BF16)], [("hid", 4096, F32)])
        hid = hid[:, :].rearrange("p (r c n) -> p r c n", r=2, c=NC)
        w_nat = w_in[:, 0:3072].rearrange("p (hh c d) -> p hh c d", c=3, d=D)
        wv_c = w_in[:, 3072:4096].rearrange("p (hh d) -> p hh d", d=D)
        wk_mem, g_hi, ctxT, k_f, q_mem1 = overlay(
            [("wk_blk", 2048, F32), ("g_hi", 2048, F32R)], [("ctxT", 1024, F32), ("k_f", 1024, F32)],
            [("q_mem1", 8192, BF16)])
        wk_blk = wk_mem[:, :].rearrange("p (hh n) -> p hh n", n=2 * D)
        q_mem = [q_mem0, q_mem1]
        q_st = [q_mem[b // 2][:, :].rearrange("p (r g n) -> p r g n", r=2, g=HP)[:, b % 2] for b in range(B)]
        px, g_lo, t_hi, t_lo = overlay([("px", 4096, F32)], [("g_lo", 2048, F32R), ("t_hi", 3072, F32R), ("t_lo", 3072, F32R)])
        G = [w[:, :].rearrange("p (h n) -> p h n", n=D) for w in (g_hi, g_lo)]
        t_ring = [w[:, :].rearrange("p (h q) -> p h q", q=S) for w in (t_hi, t_lo)]
        px = px[:, :].rearrange("p (r n) -> p r n", r=2)
        wvT, v_sb, w1_hi = overlay([("wvT", 2048, F32R), ("v_sb", 2048, F32)], [("w1_hi", 4096, F32R)])
        wvT = wvT[:, :].rearrange("p (i n) -> p i n", i=2)
        v_sb = v_sb[:, :].rearrange("p (k n) -> p k n", k=2)
        p01, w1_lo, w1_raw, w2_raw = overlay([("p01", H * S + H * P + HP * S, F32)], [("w1_lo", 4096, F32R)],
                                             [("w1_raw", 4096, F32), ("w2_raw", 4096, F32)])
        p0 = p01[:, 0:H * S].rearrange("p (h q) -> p h q", h=H)
        p1 = p01[:, H * S:H * S + H * P].rearrange("p (h q) -> p h q", h=H)
        zT = p01[:, H * S + H * P:].rearrange("p (c q) -> p c q", c=HP)
        wo_nat = p01[:, 6144:7168]
        ctx_nat = p01[:, 7168:8192].rearrange("p (t d) -> p t d", d=D)
        w1_p = [w[:, :].rearrange("p (e n) -> p e n", n=HID) for w in (w1_hi, w1_lo)]
        w2_sb = w2_raw[:, :].rearrange("p (n d) -> p n d", d=D)
        b_nat = sb("b_nat", [P, HP, 3])
        row_add = sb("row_add", [P, 3, HP])
        b_over_d = sb("b_over_d", [P, HP, 3])
        woT = sb("woT", [P, HP, D])
        n_parts = sb("n_parts", [P, 2, NT * P], F32R)
        negmax = sb("negmax", [P, 2, H])
        psums = sb("psums", [P, 2, H])
        rsum = sb("rsum", [P, 2, H])
        norm = sb("norm", [P, NT, D])
        stats = sb("stats", [P, NT, 6])
        mv = sb("mv", [P, 3, NT, 2])
        rstd = sb("rstd", [P, 3, NT])
        tmp8 = sb("tmp8", [P, 3, NT])
        negm = sb("negm", [P, 3, NT])
        k_part = sb("k_part", [P, 3, NT * P], BF16)
        k_st = sb("k_st", [P, HP, NT * P], BF16)
        v_pad = sb("v_pad", [P, NT, (DH + 1) * H + 32])
        v_heads = v_pad[:, :, 0:(DH + 1) * H].rearrange("p t (h d) -> p t h d", d=DH + 1)
        n2T = sb("n2T", [P, S])
        q_f = sb("q_f", [P, S])
        q_r = sb("q_r", [P, S])
        q_part = sb("q_part", [P, 3, S], BF16)
        mneg = sb("mneg", [P, TPB, H])
        m_f = sb("m_f", [H, S])
        m_r = sb("m_r", [H, S])
        m_part = sb("m_part", [H, 3, S], BF16)
        o_raw = sb("o_raw", [P, 4, S])
        k_r = o_raw[:, :, :].rearrange("p a n -> p (a n)")
        r_den = sb("r_den", [P, TPB, 16])
        o_n = sb("o_n", [P, TPB, D])
        oT = sb("oT", [P, S])
        wx = sb("wx", [P, 4, D])
        wqk = sb("wqk", [P, 2, D])
        bqk = sb("bqk", [P, 2])
        brow = sb("brow", [P, 3, D])
        wr_sb = sb("wr_sb", [P, NE])
        br_row = sb("br_row", [P, NE])
        b1_nat = sb("b1_nat", [NE * NC, P])
        b1T = sb("b1T", [P, NE * NC])
        b2_sb = sb("b2_sb", [NE, D])
        ident = sb("ident", [P, P])
        ident_b = sb("ident_b", [P, P], BF16)
        mask = sb("mask", [P, 4, P], BF16)
        half = sb("half", [P, NT])
        one = sb("one", [P, 1])
        score = sb("score", [P, NT, NE])
        top = sb("top", [P, NT, 8])
        top_i = sb("top_i", [P, NT, 8], U32)
        top_f = sb("top_f", [P, NT, 2])
        iota8 = sb("iota8", [P, NE])
        gate = sb("gate", [P, 4, NT])
        hot = sb("hot", [P, 2, NT, NE])
        wgt = sb("wgt", [P, NT, NE])
        wgtT = woT[0:NE, :, :].rearrange("p c d -> p (c d)")

        ps = ctx.enter_context(nc.psum_tensor("ps", [P, 8, 512], F32))

        s_x, s_bias, s_wo, s_ctx, s_wx, s_ffnb = (sem(n) for n in ("s_x", "s_bias", "s_wo", "s_ctx", "s_wx", "s_ffnb"))
        s_w = [sem(f"s_wqkv{i}") for i in range(4)]
        s_w12, s_out = [sem("s_w1"), sem("s_w2")], sem("s_out")
        s_const = sem("s_const")
        s_pool = sem("s_pool")
        s_dve = sem("s_dve")
        s_bn, s_mv, s_rstd, s_n1 = sem("s_bn"), sem("s_mv"), sem("s_rstd"), sem("s_n1")
        s_wprep = sem("s_wprep")
        s_q_sum = sem("s_q_sum")
        s_q_add, s_q_prep = sem("s_q_add"), sem("s_q_prep")
        s_set, s_set_ev, s_set_lo = sem("s_set"), sem("s_set_ev"), sem("s_set_lo")
        s_vx, s_vx_ev = sem("s_vx"), sem("s_vx_ev")
        s_xb = sem("s_xb")
        s_kpart, s_kst = sem("s_kpart"), sem("s_kst")
        s_sc, s_max, s_exp = sem("s_sc"), sem("s_max"), sem("s_exp")
        s_t, s_t_hi, s_t_lo = sem("s_t"), sem("s_t_hi"), sem("s_t_lo")
        s_v, s_v_ev = sem("s_v"), sem("s_v_ev")
        s_z, s_z_ev = sem("s_z"), sem("s_z_ev")
        s_mv2, s_n2, s_xb2 = sem("s_mv2"), sem("s_n2"), sem("s_xb2")
        s_misc, s_misc_ev = sem("s_misc"), sem("s_misc_ev")
        s_qpart, s_qfree = sem("s_qpart"), sem("s_qfree")
        s_qst = [sem(f"s_qst{b}") for b in range(B)]
        s_mst = [sem(f"s_mst{b}") for b in range(B)]
        s_mx, s_mx_ev, s_mpart = sem("s_mx"), sem("s_mx_ev"), sem("s_mpart")
        s_st, s_px, s_pv, s_pv_ev = sem("s_st"), sem("s_px"), sem("s_pv"), sem("s_pv_ev")
        s_mv3, s_n3 = sem("s_mv3"), sem("s_n3")
        s_whi, s_wlo = sem("s_whi"), sem("s_wlo")
        s_n3T, s_score, s_ed, s_wgt = sem("s_n3T"), sem("s_score"), sem("s_ed"), sem("s_wgt")
        s_h, s_ha, s_hd, s_y, s_acc = sem("s_h"), sem("s_ha"), sem("s_hd"), sem("s_y"), sem("s_acc")

        tiles = "b (i p) d -> p (b i) d"

        MAXIMA = (((2, 5), (1, 1, 1, 2, 2, 1, 1), (3, 0), (1, 1, 2, 2, 1), (3, 5)),
                  ((3, 5), (1, 2, 1, 2, 2, 1, 1), (B, 0), (1, 1, 2, 2), (B, 4)),
                  ((B, 4), (1, 3, 1, 4), (B + 1, 0), (1, 2, 2, 2), (B + 1, 3)),
                  ((B + 1, 4), (1, 3, 2, 2), (B + 2, 0), (3, 2, 3), (B + 2, 3)))

        max_plan = {}
        for b, (it, counts, it2, counts2, turn) in enumerate(MAXIMA):
            units = [("MX", b, u) for u in range(2 * HP)]
            for (i, s0), ns in ((it, counts), (it2, counts2)):
                for s, n in enumerate(ns, s0):
                    max_plan.setdefault((i, s), ([], []))[0].extend(units[:n])
                    units = units[n:]
            max_plan.setdefault(turn, ([], []))[1].append(("mT", b))
        IN_SLOT = ("V", "T", "n2T", "q", "Z", "PJ")
        BESIDE = {
            0: [("V", -1, 2), ("V", -1, 3)],
            1: [("T", 0, 4)],
            2: [("Z", -1, 2), ("T", 0, 5)],
            3: [("Z", -1, 3)],
            4: [("PJ", -1), ("T", 0, 6), ("T", 0, 7)],
            5: [("V", 0, 0)],
            6: [("n2T", -1), ("V", 0, 1), ("T", 1, 0)],
            7: [("T", 1, 1)],
            8: [("Z", 0, 0), ("T", 1, 2)],
            9: [("q", -1), ("Z", 0, 1)],
            10: [("T", 1, 3)],
        }
        slots = [[("T", 0, 0)], [("T", 0, 1)]]
        for b in range(B):
            at = {s: [(kind, b + db, *n) for kind, db, *n in units if 0 <= b + db < B] for s, units in BESIDE.items()}
            if b == 0:
                at = {s: [k for k in units if k not in (("T", 0, 4), ("T", 0, 5))] for s, units in at.items()}
                for s, u in zip((0, 1, 2, 2), range(2, 6)):
                    at.setdefault(s, []).append(("T", 0, u))
            for s in range(12):
                slot = [("S", b, s)]
                units = sorted(at.get(s, []), key=lambda k: IN_SLOT.index(k[0]))
                if b == 0 and s < 10:
                    units += [("P", 0, s)]
                maxima_now, turn = max_plan.get((b, s), ([], []))
                units = maxima_now[:1] + units + maxima_now[1:] + turn
                slots.append(slot + units)
        last = B - 1
        for b in range(B):
            units = [("oq0", b - 1), ("oT0", b - 1), ("oq1", b - 1), ("oT1", b - 1), ("wo", b - 1)] if b else \
                [("V", last, 2), ("V", last, 3), ("Z", last, 2), ("Z", last, 3), ("PJ", last), ("n2T", last), ("q", last)]
            tail = {}
            for g, unit in zip((2, 3, 4, 5, 5) if b else (0, 0, 1, 2, 3, 5, 6), units):
                tail.setdefault(g, []).append(unit)
            more = {(2, 1): [("b1", 0)], (3, 1): [("NT", 0)], (3, 7): [("RT", 0)]}
            for g in range(HP):
                maxima_now, turn = max_plan.get((B + b, g), ([], []))
                slot = [("CS", b, g, 0)] + maxima_now[:1] + [("CS", b, g, 1)]
                if b == 0:
                    slot += tail.get(g, [])
                if g in (2, 4, 6):
                    slot += [("CO", b, g // 2 - 1)]
                if g == 0 and b >= 1:
                    slot += [("CO", b - 1, 3)]
                slot += maxima_now[1:2] + (tail.get(g, []) if b else []) + maxima_now[2:] + more.get((b, g), []) + turn
                if b == 2:
                    slot += [("WS", 0, g)]
                slots.append(slot)
        slots.append([("CO", last, 3)])
        extra = {0: [("GT", 0), ("oq0", last)], 1: [("WT", 0), ("oT0", last)], 2: [("B2", 0), ("oq1", last)], 3: [("oT1", last), ("wo", last)],
                 5: [("NT", 1)], 6: [("RT", 1)], 7: [("GT", 1)], 8: [("WT", 1)], 9: [("B2", 1)]}
        for k in range(2 * NE):
            more = extra.get(k, []) + [None, None]
            units = [("H", k, 0), more[0], ("H", k, 1), ("H", k, 2), more[1], ("H", k, 3)]
            slots.append([u for u in units if u] + ([("Y", k - 1)] if k else []))
        slots.append([("Y", 2 * NE - 1)])
        MISC = ("PJ", "n2T", "q", "mT", "oq0", "oT0", "oq1", "oT1", "wo", "b1", "NT", "RT", "WT", "B2")
        misc_at = {k: i for i, k in enumerate(k for slot in slots for k in slot if k[0] in MISC)}
        ring = [k for slot in slots for k in slot if k[0] in "TVZ"]
        ring_bank = {k: 3 + i % 3 for i, k in enumerate(ring)}
        G_BANK, H_BANK, Y_BANK = (0, 1, 2, 5), (0, 1, 2, 5), (6, 3)

        flat = [k for slot in slots for k in slot]

        def accumulated(hf):
            return sum(k[0] == "Y" for k in flat[:flat.index(("B2", hf))])

        max_bank, max_before, in_bank = {}, {}, {}
        z_all = flat.index(("Z", B - 1, 3))
        for at, key in enumerate(flat):
            if key[0] == "MX":
                n = len(max_bank)
                bank = 6 if at < z_all or n % 2 == 0 else 5
                max_bank[key], max_before[key], in_bank[bank] = bank, in_bank.get(bank, 0), n + 1
        first_in_5 = next(k for k in max_bank if max_bank[k] == 5)

        N1T_OUT = 6
        KEYS_OUT = N1T_OUT + 8

        block = ctx.enter_context(nc.Block())

        def split(eng, step, dst, src, rest, done, before):
            eng.tensor_copy(dst[0], src).then_inc(done, 1)
            eng.wait_ge(done, before + 1)
            step(eng.tensor_tensor(rest, src, dst[0], ALU.subtract))
            eng.tensor_copy(dst[1], rest).then_inc(done, 1)
            eng.wait_ge(done, before + 2)
            eng.tensor_tensor(dst[2], rest, dst[1], ALU.subtract).then_inc(done, 1)

        def split_q(eng, step, b):
            eng.wait_ge(s_misc_ev, misc_at[("q", b)] + 1)
            if b >= 1:
                eng.wait_ge(s_qst[b - 1], 16 * 12)
            split(eng, step, [q_part[:, i, :] for i in range(3)], q_f[:, :], q_r[:, :], s_qpart, 3 * b)

        def split_m(eng, step, b):
            eng.wait_ge(s_misc_ev, misc_at[("mT", b)] + 1)
            if b >= 1:
                eng.wait_ge(s_mst[b - 1], 16 * 6)
            split(eng, step, [m_part[:, i, :] for i in range(3)], m_f[:, :], m_r[:, :], s_mpart, 3 * b)

        @block.sync
        def _(sp):
            sp.dma_start(resid[:, :, :], x.rearrange(tiles, p=P)).then_inc(s_x, 16)
            w_view = w_qkv.rearrange("(hh p c) d -> p hh (c d)", p=P, c=3)
            sp.dma_start(b_nat[:, :, :], b_qkv.rearrange("(hh p c) -> p hh c", p=P, c=3)).then_inc(s_bias, 16)
            for i in range(4):
                sp.dma_start(w_in[:, 768 * i:768 * (i + 1)].rearrange("p (hh n) -> p hh n", hh=2),
                             w_view[:, 2 * i:2 * i + 2, :]).then_inc(s_w[i], 16)
            sp.dma_start(wo_nat, w_o).then_inc(s_wo, 16)
            sp.dma_start(ctx_nat, ctx_in.rearrange(tiles, p=P)).then_inc(s_ctx, 16)
            for i, w in enumerate((wq, wk, wv, wo)):
                sp.dma_start(wx[:, i, :], w).then_inc(s_wx, 16)
            with nc.allow_non_contiguous_dma(reason="128 biases, in the order of the permuted columns"):
                for i, v in enumerate((bq, bk)):
                    for par in range(2):
                        sp.dma_start(bqk[64 * par:64 * par + 64, i:i + 1],
                                      v[64 * par:64 * par + 64].rearrange("(g d) -> d g", d=DH)).then_inc(s_ffnb, 16)
            for i, v in enumerate((b_o, bv, bo)):
                sp.dma_start(brow[:, i, :], v.partition_broadcast(P)).then_inc(s_wx, 16)
            sp.dma_start(br_row[:, :], br.partition_broadcast(P)).then_inc(s_wx, 16)
            sp.dma_start(wr_sb[:, :], wr).then_inc(s_wx, 16)
            sp.dma_start(b1_nat[:, :], b1.rearrange("e (c p) -> (e c) p", p=P)).then_inc(s_ffnb, 16)
            sp.dma_start(b2_sb[:, :], b2).then_inc(s_ffnb, 16)
            sp.wait_ge(s_kpart, 3)
            sp.wait_ge(s_const, 5)
            for par in range(2):
                for n, part in enumerate(PARTS_K):
                    r = 64 * par + DH * n
                    sp.dma_start(k_st[r:r + DH, :, :], k_part[64 * par:64 * par + 64, part, :]).then_inc(s_kst, 16)

            def stack_q(b):
                sp.wait_ge(s_qpart, 3 * (b + 1))
                sp.wait_ge(s_qfree, b // 2 + 1)
                for par in range(2):
                    for n, part in enumerate(PARTS_Q):
                        r = 64 * par + DH * n
                        sp.dma_start(q_st[b][r:r + DH, :, S * par:S * par + S],
                                     q_part[64 * par:64 * par + 64, part, :]
                                     ).then_inc(s_qst[b], 16)

            def stack_m(b):
                sp.wait_ge(s_mpart, 3 * (b + 1))
                for par in range(2):
                    for part in range(3):
                        r = 64 * par + MAX_ROW + part
                        sp.dma_start(q_st[b][r:r + 1, :, S * par:S * par + S],
                                     m_part[8 * par:8 * par + 8, part, :]).then_inc(s_mst[b], 16)

            stack_q(0)
            stack_q(1)
            stack_m(0)
            stack_q(2)
            stack_m(1)
            stack_q(3)
            sp.wait_ge(s_misc, misc_at[("PJ", B - 1)] + 1)
            sp.dma_start(w1_raw[:, :].rearrange("p (e n) -> p e n", n=HID), w1.rearrange("e p n -> p e n")
                         ).then_inc(s_w12[0], 16)
            stack_m(2)
            sp.dma_start(w2_sb, w2.rearrange("e (c p) d -> p (e c) d", p=P)).then_inc(s_w12[1], 16)
            stack_m(3)
            for hf in range(2):
                sp.wait_ge(s_acc, NE * (hf + 1))
                sp.dma_start(out.rearrange(tiles, p=P)[:, 4 * hf:4 * hf + 4, :],
                             resid[:, 4 * hf:4 * hf + 4, :]).then_inc(s_out, 16)
            sp.wait_ge(s_out, 32)

        @block.gpsimd
        def _(pool):
            steps = [0]

            def step(ins):
                steps[0] += 1
                ins.then_inc(s_pool, 1)
                pool.wait_ge(s_pool, steps[0])

            step(pool.memset(ident_b[:, :], 0.0))
            pool.affine_select(out=ident_b[:, :], in_=ident_b[:, :], compare_op=ALU.not_equal, fill=1.0, base=0,
                               pattern=[[-1, P]], channel_multiplier=1).then_inc(s_const, 1)
            step(pool.memset(mask[:, :, :], 0.0))
            pool.affine_select(out=mask[:, :, :], in_=mask[:, :, :], compare_op=ALU.is_ge, fill=MASKED, base=0,
                               pattern=[[0, 4], [1, P]], channel_multiplier=-1).then_inc(s_const, 1)
            pool.memset(one[:, :], 1.0)
            pool.memset(wk_mem[:, :], 0.0).then_inc(s_const, 1)
            step(pool.memset(ident[:, :], 0.0))
            pool.affine_select(out=ident[:, :], in_=ident[:, :], compare_op=ALU.not_equal, fill=1.0, base=0,
                               pattern=[[-1, P]], channel_multiplier=1).then_inc(s_const, 1)
            step(pool.memset(half[:, :], -0.5))

            def rsqrt_of_var(n, t0, cnt):
                step(pool.tensor_scalar(tmp8[:, n, t0:t0 + cnt], mv[:, n, t0:t0 + cnt, 1], EPS_LN, None, ALU.add))
                step(pool.tensor_tensor(rstd[:, n, t0:t0 + cnt], tmp8[:, n, t0:t0 + cnt], half[:, 0:cnt], ALU.pow))
                step(pool.tensor_scalar(negm[:, n, t0:t0 + cnt], mv[:, n, t0:t0 + cnt, 0], -1.0, None, ALU.mult))

            pool.wait_ge(s_mv, NT)
            step(pool.tensor_scalar(tmp8[:, 0, :], mv[:, 0, :, 1], EPS_LN, EPS_RMS, ALU.add, ALU.mult))
            step(pool.tensor_tensor(tmp8[:, 0, :], tmp8[:, 0, :], mv[:, 0, :, 1], ALU.add))
            step(pool.tensor_scalar(negm[:, 0, :], mv[:, 0, :, 0], -1.0, None, ALU.mult))
            pool.tensor_tensor(rstd[:, 0, :], tmp8[:, 0, :], half[:, :], ALU.pow).then_inc(s_rstd, 1)

            pool.memset(k_st[:, :, :].bitcast(F32), TWO_ONES).then_inc(s_const, 1)
            pool.memset(v_pad[:, :, :], 1.0).then_inc(s_const, 1)
            pool.iota(iota8[:, :], pattern=[[1, NE]], base=0, channel_multiplier=0,
                      allow_small_or_imprecise_dtypes=True).then_inc(s_const, 1)

            pool.wait_ge(s_wx, 144)
            pool.tensor_copy(wqk[:, :, :].rearrange("p i (r d g) -> p (i r) d g", r=2, d=DH),
                             wx[:, 0:2, :].rearrange("p i (r g d) -> p (i r) d g", r=2, d=DH)).then_inc(s_const, 1)
            pool.wait_ge(s_n1, NT)
            pool.wait_ge(s_wx, 144)
            pool.tensor_tensor(resid[:, :, :], resid[:, :, :],
                               brow[:, 0:1, :].to_broadcast([P, NT, D]), ALU.add).then_inc(s_xb, 1)
            pool.wait_ge(s_set_ev, KEYS_OUT)
            split(pool, step, [k_part[:, i, :] for i in range(3)], k_f[:, :], k_r, s_kpart, 0)
            pool.memset(q_mem0[:, :].bitcast(F32), 0.0).then_inc(s_qfree, 1)

            def norm_batch(n, b, s_in, s_norm):
                pool.wait_ge(s_in, TPB * (b + 1))
                rsqrt_of_var(n, TPB * b, TPB)
                for t in range(TPB * b, TPB * b + TPB):
                    pool.tensor_scalar(norm[:, t, :], resid[:, t, :], negm[:, n, t:t + 1], rstd[:, n, t:t + 1],
                                       ALU.add, ALU.mult).then_inc(s_norm, 1)

            def norm_2(b):
                norm_batch(1, b, s_mv2, s_n2)
                pool.wait_ge(s_n2, TPB * (b + 1))
                pool.tensor_tensor(resid[:, TPB * b:TPB * b + TPB, :], resid[:, TPB * b:TPB * b + TPB, :],
                                   brow[:, 2:3, :].to_broadcast([P, TPB, D]), ALU.add).then_inc(s_xb2, 1)

            def norm_3(b):
                norm_batch(2, b, s_mv3, s_n3)

            norm_2(0)
            split_q(pool, step, 0)
            norm_2(1)
            split_q(pool, step, 1)
            norm_2(2)
            pool.wait_ge(s_t_lo, HP * B)
            pool.memset(q_mem1[:, :].bitcast(F32), 0.0).then_inc(s_qfree, 1)
            split_m(pool, step, 0)
            split_q(pool, step, 2)
            norm_2(3)
            norm_3(0)
            norm_3(1)
            norm_3(2)
            norm_3(3)
        @block.tensor
        def _(pe):
            pe.wait_ge(s_const, 2)
            for _ in range(WARM_UP):
                pe.matmul(ps[:, 7, :], ident_b[:, :], mask[:, :, :], start=True, stop=True)
            pe.wait_ge(s_const, 4)
            def g_pairs(i):
                pe.wait_ge(s_wprep, 2 * i + 2)
                pe.wait_ge(s_q_prep, 2 * i + 2)
                for hh in (2 * i, 2 * i + 1):
                    last = pe.matmul(ps[:, G_BANK[i], 256 * (hh % 2):256 * (hh % 2) + 256], w_nat[:, hh, 0, :],
                                     wk_blk[:, hh, :], start=True, stop=True)
                last.then_inc(s_set, 1)

            g_pairs(0)
            g_pairs(1)
            for t in range(NT):
                pe.wait_ge(s_n1, t + 1)
                last = pe.transpose(ps[:, 6 + t // 4, P * (t % 4):P * (t % 4) + P], norm[:, t, :], ident[:, :])
                if t % 4 == 3:
                    last.then_inc(s_set, 1)
            g_pairs(2)
            g_pairs(3)
            def products(out, a, b_):
                pe.matmul(out, a[0], b_[0], start=True, stop=False)
                pe.matmul(out, a[1], b_[0], start=False, stop=False)
                return pe.matmul(out, a[0], b_[1], start=False, stop=True)

            def ring_free(key):
                k = ring.index(key)
                if k >= 3:
                    kind, b, i = ring[k - 3]
                    if kind == "T":
                        pe.wait_ge(s_t_lo, HP * b + i + 1)
                    elif kind == "V":
                        pe.wait_ge(s_v_ev, 4 * b + i + 1)
                    else:
                        pe.wait_ge(s_z_ev, 4 * b + i + 1)
                return ps[:, ring_bank[key], :]

            def n_of(c0, n):
                return [n_parts[:, i, c0:c0 + n] for i in range(2)]

            def t_of(b, u):
                if b == 0 and u < 3:
                    pe.wait_ge(s_set_lo, (2, 2, 5)[u])
                bank = ring_free(("T", b, u))
                for h in (2 * u, 2 * u + 1):
                    last = products(bank[:, S * (h % 2):S * (h % 2) + S], [g[:, h, :] for g in G], n_of(S * b, S))
                last.then_inc(s_t, 1)

            def prepare(n):
                bank = 6 + n % 2
                if n == 0:
                    pe.wait_ge(s_set_lo, 6)
                    pe.wait_ge(s_wo, 16)
                if n == 2:
                    pe.wait_ge(s_wprep, 9)
                if n >= 2:
                    pe.wait_ge(s_set_ev, N1T_OUT + n - 1)
                elif n == 1:
                    pe.wait_ge(s_set_ev, N1T_OUT)
                cols = ps[:, bank, :].rearrange("p (c n) -> p c n", n=P)
                if n in (4, 5):
                    pe.wait_ge(s_set_lo, n + 3)
                if n == 4:
                    pe.wait_ge(s_ctx, 16)
                if n == 6:
                    pe.wait_ge(s_wx, 144)
                    pe.wait_ge(s_const, 8)
                for c in range(4):
                    m = 4 * (n % 2) + c
                    if n < 2:
                        last = pe.transpose(cols[:, c, :], wo_nat[:, P * m:P * m + P], ident[:, :])
                    elif n < 4:
                        last = pe.transpose(cols[:, c, :], wv_c[:, m, :], ident[:, :])
                    elif n < 6:
                        last = pe.transpose(cols[:, c, :], ctx_nat[:, m, :], ident[:, :])
                    elif n < 8:
                        if c == 0:
                            last = pe.matmul(ps[:, bank, :], wqk[:, 1, :], ctxT[:, 512 * (n % 2):512 * (n % 2) + 512],
                                             start=True, stop=True)
                    else:
                        last = pe.matmul(cols[:, c, :], ctxT[:, P * m:P * m + P], wx[:, 2, :], start=True, stop=True)
                last.then_inc(s_set if n < 8 else s_vx, 1)

            def scores(b, s):
                k = 12 * b + s
                ge(pe, s_exp, k - 2)
                bank = ps[:, k % 3, :]
                if s % 3 < 2:
                    u = HP * b + 2 * (s // 3) + s % 3
                    pe.wait_ge(s_t_lo, u + 1)
                    for a, t in ((0, 0), (1, 0), (0, 1)):
                        pe.matmul(bank, n_parts[:, a, S * b:S * b + P], t_ring[t][:, 2 * (u % 6):2 * (u % 6) + 2, :],
                                  start=(a + t == 0), stop=False)
                    pe.matmul(bank.rearrange("p (h q) -> p h q", h=2)[:, :, 0:P], ident_b[:, :], mask[:, 0:2, :],
                              start=False, stop=True).then_inc(s_sc, 1)
                else:
                    u = HP * b + 2 * (s // 3)
                    for a, t in ((0, 0), (1, 0), (0, 1)):
                        pe.matmul(bank, n_parts[:, a, S * b + P:S * b + S], t_ring[t][:, 2 * (u % 6):2 * (u % 6) + 4, P:S],
                                  start=(a + t == 0), stop=False)
                    pe.matmul(bank, ident_b[:, :], mask[:, :, :], start=False, stop=True).then_inc(s_sc, 1)

            def values(b, i):
                if b == 0 and i == 0:
                    pe.wait_ge(s_set_ev, N1T_OUT + 4)
                    pe.wait_ge(s_set_lo, 8)
                bank = ring_free(("V", b, i))
                kt, hf = i % 2, i // 2
                products(bank, n_of(S * b + P * kt, P), [wvT[:, j, 512 * hf:512 * hf + 512] for j in range(2)]
                         ).then_inc(s_v, 1)

            def heads_out(b, zu):
                bank = ring_free(("Z", b, zu))
                pe.wait_ge(s_exp, 12 * b + 3 * zu + 3)
                pe.wait_ge(s_v_ev, 4 * b + 2 * (zu // 2) + 2)
                for pair in (2 * zu, 2 * zu + 1):
                    c0 = S * (pair % 2)
                    for kt in range(2):
                        for hp in range(2):
                            h = 2 * pair + hp
                            v = v_sb[:, kt, E1 * h:E1 * h + E1]
                            o = bank[64 * hp:64 * hp + 64, c0:c0 + S]
                            if kt == 0:
                                last = pe.matmul(o, v, p0[:, h, :], start=True, stop=False)
                            else:
                                last = pe.matmul(o[:, P:S], v, p1[:, h, :], start=False, stop=True)
                last.then_inc(s_z, 1)

            def project(b):
                if b == 0:
                    pe.wait_ge(s_set_ev, N1T_OUT + 2)
                misc(("PJ", b))
                pe.wait_ge(s_z_ev, 4 * b + 4)
                for i in range(TPB):
                    for c in range(HP):
                        last = pe.matmul(ps[:, 7, P * i:P * i + P], zT[:, c, P * i:P * i + P], woT[:, c, :],
                                         start=(c == 0), stop=(c == HP - 1))
                last.then_inc(s_misc, 1)

            def misc(key):
                if misc_at[key] == 0:
                    pe.wait_ge(s_vx_ev, 2)
                ge(pe, s_misc_ev, misc_at[key])

            def query(b, n):
                if n == 0:
                    misc(("n2T", b))
                    pe.wait_ge(s_n2, TPB * (b + 1))
                    for i in range(TPB):
                        last = pe.transpose(ps[:, 7, P * i:P * i + P], norm[:, TPB * b + i, :], ident[:, :])
                else:
                    misc(("q", b))
                    last = pe.matmul(ps[:, 7, 0:S], wqk[:, 0, :], n2T[:, :], start=True, stop=True)
                last.then_inc(s_misc, 1)

            def max_scores(b, u):
                g, qt = u // 2, u % 2
                if u == 0:
                    pe.wait_ge(s_qst[b], 16 * 12)
                    if b == 0:
                        pe.wait_ge(s_kst, 16 * 12)
                        pe.wait_ge(s_vx_ev, 1)
                if ("MX", b, u) == first_in_5:
                    pe.wait_ge(s_z_ev, 4 * B)
                ge(pe, s_mx_ev, max_before[("MX", b, u)])
                for par in range(2):
                    last = pe.matmul(ps[:, max_bank[("MX", b, u)], S * par:S * par + S],
                                     q_st[b][:, g, S * par + P * qt:S * par + P * qt + P],
                                     k_st[:, g, S * b:S * b + S], start=True, stop=True)
                last.then_inc(s_mx, 1)

            def max_turn(b):
                misc(("mT", b))
                pe.wait_ge(s_mx_ev, 16 * b + 16)
                for i in range(TPB):
                    last = pe.transpose(ps[0:H, 7, P * i:P * i + P], mneg[:, i, :], ident[:, :])
                last.then_inc(s_misc, 1)

            def cross_scores(b, g, kt):
                if g == 0 and kt == 0:
                    pe.wait_ge(s_mst[b], 16 * 6)
                k = 2 * (HP * b + g) + kt
                if k < 3:
                    pe.wait_ge(s_exp, 12 * B - 2 + k)
                else:
                    pe.wait_ge(s_px, k - 2)
                pe.matmul(ps[:, k % 3, :], k_st[:, g, S * b + P * kt:S * b + P * kt + P], q_st[b][:, g, :],
                          start=True, stop=True).then_inc(s_st, 1)

            def cross_out(b, g4):
                pe.wait_ge(s_px, 16 * b + 4 * g4 + 4)
                m = 2 * b + g4 // 2
                if m < 2:
                    pe.wait_ge(s_z_ev, 4 * B)
                else:
                    pe.wait_ge(s_pv_ev, m - 1)
                for kt in range(2):
                    for j in range(4):
                        h = 2 * g4 + j // 2 + 8 * (j % 2)
                        p = px[:, g4 % 2, 1024 * (j // 2) + 512 * kt + S * (j % 2):][:, 0:S]
                        last = pe.matmul(ps[32 * j:32 * j + 32, 3 + m % 2, S * (g4 % 2):S * (g4 % 2) + S],
                                         v_pad[:, TPB * b + kt, (DH + 1) * h:(DH + 1) * h + 32], p, start=(kt == 0), stop=(kt == 1))
                last.then_inc(s_pv, 1)

            def out_step(b, n):
                if n in (0, 2):
                    qt = n // 2
                    misc((f"oq{qt}", b))
                    pe.wait_ge(s_pv_ev, 2 * b + 2)
                    for g4 in range(4):
                        last = pe.transpose(ps[:, 7, P * g4:P * g4 + P], o_raw[:, g4, P * qt:P * qt + P], ident[:, :])
                elif n in (1, 3):
                    qt = n // 2
                    misc((f"oT{qt}", b))
                    last = pe.transpose(ps[:, 7, 0:P], o_n[:, qt, :], ident[:, :])
                else:
                    misc(("wo", b))
                    for i in range(TPB):
                        last = pe.matmul(ps[:, 7, P * i:P * i + P], oT[:, P * i:P * i + P], wx[:, 3, :],
                                         start=True, stop=True)
                last.then_inc(s_misc, 1)

            def expert_step(kind, hf):
                misc((kind, hf))
                ts = range(4 * hf, 4 * hf + 4)
                if kind == "b1":
                    pe.wait_ge(s_ffnb, 96)
                    last = pe.transpose(ps[:, 7, 0:NE * NC], b1_nat[:, :], ident[0:NE * NC, 0:NE * NC])
                elif kind == "NT":
                    pe.wait_ge(s_n3, 4 * hf + 4)
                    for t in ts:
                        last = pe.transpose(ps[:, 7, P * (t % 4):P * (t % 4) + P], norm[:, t, :], ident[:, :])
                elif kind == "RT":
                    for t in ts:
                        for i in range(2):
                            last = pe.matmul(ps[:, 7, NE * (t % 4):NE * (t % 4) + NE],
                                             n_parts[:, i, P * t:P * t + P].bitcast(F32), wr_sb[:, :],
                                             start=(i == 0), stop=(i == 1))
                elif kind == "WT":
                    pe.wait_ge(s_wgt, hf + 1)
                    for t in ts:
                        last = pe.transpose(ps[0:NE, 7, P * (t % 4):P * (t % 4) + P], wgt[:, t, :], ident[:, :])
                else:
                    for t in ts:
                        last = pe.matmul(ps[:, 7, P * (t % 4):P * (t % 4) + P], wgtT[:, P * t:P * t + P],
                                         b2_sb[:, :], start=True, stop=True)
                last.then_inc(s_misc, 1)

            def hidden(k, c):
                e, hf = k % NE, k // NE
                if k == 0 and c == 0:
                    pe.wait_ge(s_wlo, 8)
                    pe.wait_ge(s_px, 16 * B)
                    pe.wait_ge(s_mx_ev, 16 * B)
                if k % NE == 0 and c == 0:
                    pe.wait_ge(s_misc_ev, misc_at[("NT", hf)] + 1)
                if k >= 1:
                    pe.wait_ge(s_ha if c % 2 == 0 else s_hd, 2 * (k - 1) + c // 2 + 1)
                products(ps[:, H_BANK[c], :], [w[:, e, P * c:P * c + P] for w in w1_p], n_of(512 * hf, 512)).then_inc(s_h, 1)

            def combine(k):
                e = k % NE
                if k == 0:
                    pe.wait_ge(s_w12[1], 16)
                    pe.wait_ge(s_pv_ev, 2 * B)
                ge(pe, s_acc, k - 1)
                pe.wait_ge(s_ha, 2 * k + 2)
                pe.wait_ge(s_hd, 2 * k + 2)
                for tt in range(4):
                    for c in range(NC):
                        last = pe.matmul(ps[:, Y_BANK[k % 2], P * tt:P * tt + P], hid[:, k % 2, c, P * tt:P * tt + P],
                                         w2_sb[:, NC * e + c, :], start=(c == 0), stop=(c == NC - 1))
                last.then_inc(s_y, 1)

            for slot in slots:
                for kind, b, *i in slot:
                    if kind == "S":
                        scores(b, *i)
                    elif kind == "T":
                        t_of(b, *i)
                    elif kind == "V":
                        values(b, *i)
                    elif kind == "Z":
                        heads_out(b, *i)
                    elif kind == "P":
                        prepare(*i)
                    elif kind == "PJ":
                        project(b)
                    elif kind in ("n2T", "q"):
                        query(b, kind == "q")
                    elif kind == "MX":
                        max_scores(b, *i)
                    elif kind == "mT":
                        max_turn(b)
                    elif kind == "CS":
                        cross_scores(b, *i)
                    elif kind == "CO":
                        cross_out(b, *i)
                    elif kind in ("oq0", "oT0", "oq1", "oT1", "wo"):
                        out_step(b, ("oq0", "oT0", "oq1", "oT1", "wo").index(kind))
                    elif kind == "H":
                        hidden(b, *i)
                    elif kind == "Y":
                        combine(b)
                    elif kind in ("b1", "NT", "RT", "WT", "B2"):
                        expert_step(kind, b)


        @block.scalar
        def _(act):
            def copy_out(n, dst, src):
                act.wait_ge(s_set, n + 1)
                act.copy(dst, src).then_inc(s_set_ev, 1)

            def q_sums(i):
                act.wait_ge(s_w[i], 16)
                for hh in (2 * i, 2 * i + 1):
                    act.activation(p01[:, D * hh:D * hh + D], w_nat[:, hh, 0, :], ACT.Identity,
                                   accum_out=row_add[:, 0, hh:hh + 1]).then_inc(s_q_sum, 1)

            def q_weights(i):
                act.wait_ge(s_q_add, i + 1)
                for hh in (2 * i, 2 * i + 1):
                    act.activation(w_nat[:, hh, 0, :], w_nat[:, hh, 0, :], ACT.Identity, bias=row_add[:, 0, hh:hh + 1]
                                   ).then_inc(s_q_prep, 1)

            def g_out(i, n):
                copy_out(n, G[0][:, 4 * i:4 * i + 4, :], ps[:, G_BANK[i], :])

            def n_out(i):
                act.wait_ge(s_set, 3 + i)
                act.activation(n_parts[:, 0, 512 * i:512 * i + 512], ps[:, 6 + i, :], ACT.Identity, bias=one[:, 0:1]
                               ).then_inc(s_set_ev, 1)

            q_sums(0)
            q_sums(1)
            q_weights(0)
            q_weights(1)
            q_sums(2)
            q_sums(3)
            g_out(0, 0)
            g_out(1, 1)
            act.wait_ge(s_const, 3)
            n_out(0)
            q_weights(2)
            n_out(1)
            q_weights(3)
            g_out(2, 4)
            g_out(3, 5)

            def prepared(n):
                i = n % 2
                cols = slice(512 * i, 512 * i + 512)
                if n < 6:
                    dst = (woT[:, 4 * i:4 * i + 4, :], wvT[:, 0, cols], ctxT[:, cols])[n // 2]
                    copy_out(N1T_OUT + n, dst, ps[:, 6 + i, :])
                elif n < 8:
                    if n == 6:
                        act.wait_ge(s_ffnb, 96)
                    act.wait_ge(s_set, N1T_OUT + n + 1)
                    act.activation(k_f[:, cols], ps[:, 6 + i, :], ACT.Identity, bias=bqk[:, 1:2]).then_inc(s_set_ev, 1)

            def t_high(b, u):
                k = HP * b + u
                act.wait_ge(s_t, k + 1)
                if k >= 6:
                    last_use = k - 6
                    act.wait_ge(s_sc, 12 * (last_use // HP) + 3 * (last_use % HP // 2) + 3)
                bank = ps[:, ring_bank[("T", b, u)], :]
                act.copy(t_ring[0][:, 2 * (k % 6):2 * (k % 6) + 2, :], bank.rearrange("p (h q) -> p h q", h=2)
                         ).then_inc(s_t_hi, 1)

            def probabilities(b, u):
                k = 12 * b + u
                act.wait_ge(s_max, k + 1)
                bank = ps[:, k % 3, :]
                j = u // 3
                if u % 3 < 2:
                    heads, kt, n = range(4 * j + 2 * (u % 3), 4 * j + 2 * (u % 3) + 2), 0, S
                else:
                    heads, kt, n = range(4 * j, 4 * j + 4), 1, P
                for i, h in enumerate(heads):
                    dst = p0[:, h, :] if kt == 0 else p1[:, h, :]
                    last = act.activation(dst, bank[:, n * i:n * i + n], ACT.Exp, bias=negmax[:, kt, h:h + 1],
                                          accum_out=psums[:, kt, h:h + 1])
                last.then_inc(s_exp, 1)

            def query_out(b, n):
                if n == 0:
                    act.wait_ge(s_misc, misc_at[("n2T", b)] + 1)
                    act.copy(n2T[:, :], ps[:, 7, 0:S]).then_inc(s_misc_ev, 1)
                    return
                act.wait_ge(s_misc, misc_at[("q", b)] + 1)
                ge(act, s_qpart, 3 * b)
                act.activation(q_f[:, :], ps[:, 7, 0:S], ACT.Identity, bias=bqk[:, 0:1]).then_inc(s_misc_ev, 1)

            def max_out(b):
                act.wait_ge(s_misc, misc_at[("mT", b)] + 1)
                ge(act, s_mpart, 3 * b)
                act.copy(m_f[:, :], ps[0:H, 7, 0:S]).then_inc(s_misc_ev, 1)

            def z_out(b, i):
                act.wait_ge(s_z, 4 * b + i + 1)
                if b >= 1:
                    act.wait_ge(s_misc, misc_at[("PJ", b - 1)] + 1)
                act.copy(zT[:, 2 * i:2 * i + 2, :], ps[:, ring_bank[("Z", b, i)], :]).then_inc(s_z_ev, 1)

            def cross_probabilities(b, g, kt):
                k = 2 * (HP * b + g) + kt
                act.wait_ge(s_st, k + 1)
                ge(act, s_pv, 4 * b + g // 2 - 1)
                c0 = 1024 * (g % 2) + 512 * kt
                act.activation(px[:, (g // 2) % 2, c0:c0 + 512], ps[:, k % 3, :], ACT.Exp,
                               scale=SCALE_X).then_inc(s_px, 1)

            def cross_copy(b, i):
                act.wait_ge(s_pv, 4 * b + 2 * i + 2)
                if b == 0 and i == 0:
                    act.wait_ge(s_kpart, 3)
                if i == 0:
                    ge(act, s_misc, misc_at[("oq1", b - 1)] + 1 if b else 0)
                act.copy(o_raw[:, 2 * i:2 * i + 2, :], ps[:, 3 + i, :]).then_inc(s_pv_ev, 1)

            def out_copy(b, qt):
                act.wait_ge(s_misc, misc_at[(f"oT{qt}", b)] + 1)
                act.copy(oT[:, P * qt:P * qt + P], ps[:, 7, 0:P]).then_inc(s_misc_ev, 1)

            def weight_high(i):
                act.wait_ge(s_w12[0], 16)
                act.copy(w1_hi[:, 512 * i:512 * i + 512], w1_raw[:, 512 * i:512 * i + 512]).then_inc(s_whi, 1)

            def relu(k, c):
                act.wait_ge(s_h, 4 * k + c + 1)
                ge(act, s_y, k - 1)
                act.activation(hid[:, k % 2, c, :], ps[:, H_BANK[c], :], ACT.Relu,
                               bias=b1T[:, NC * (k % NE) + c:NC * (k % NE) + c + 1]).then_inc(s_ha, 1)

            def expert_copy(kind, hf):
                cols = slice(512 * hf, 512 * hf + 512)
                if kind == "RT":
                    act.wait_ge(s_score, 2 * hf + 2)
                    act.activation(gate[:, 1, 4 * hf:4 * hf + 4], gate[:, 0, 4 * hf:4 * hf + 4], ACT.Exp).then_inc(s_ed, 1)
                    return
                act.wait_ge(s_misc, misc_at[(kind, hf)] + 1)
                if kind == "b1":
                    act.copy(b1T[:, :], ps[:, 7, 0:NE * NC]).then_inc(s_misc_ev, 1)
                elif kind == "NT":
                    act.copy(n_parts[:, 0, cols], ps[:, 7, :]).then_inc(s_n3T, 1)
                else:
                    act.copy(wgtT[:, cols], ps[0:NE, 7, :]).then_inc(s_misc_ev, 1)

            for slot in slots:
                for kind, b, *i in slot:
                    if kind == "T":
                        t_high(b, *i)
                for kind, b, *i in slot:
                    if kind == "S":
                        probabilities(b, *i)
                    elif kind == "Z":
                        z_out(b, *i)
                    elif kind == "P" and i[0] < 8:
                        prepared(*i)
                    elif kind in ("n2T", "q"):
                        query_out(b, kind == "q")
                    elif kind == "mT":
                        max_out(b)
                    elif kind == "CS":
                        cross_probabilities(b, *i)
                    elif kind == "CO" and i[0] % 2 == 1:
                        cross_copy(b, i[0] // 2)
                    elif kind in ("oT0", "oT1"):
                        out_copy(b, int(kind == "oT1"))
                    elif kind == "WS":
                        weight_high(*i)
                    elif kind == "H" and i[0] % 2 == 0:
                        relu(b, *i)
                    elif kind in ("b1", "NT", "RT", "WT"):
                        expert_copy(kind, b)

        @block.vector
        def _(dve):
            steps = [0]

            def step(ins):
                steps[0] += 1
                ins.then_inc(s_dve, 1)
                dve.wait_ge(s_dve, steps[0])

            dve.wait_ge(s_x, 16)
            for t in range(NT):
                dve.bn_stats(stats[:, t, :], resid[:, t, :]).then_inc(s_bn, 1)
            dve.wait_ge(s_bn, NT)
            for t in range(NT):
                dve.bn_aggr(mv[:, 0, t, :], stats[:, t, :]).then_inc(s_mv, 1)

            def first_norm():
                dve.wait_ge(s_rstd, 1)
                for t in range(NT):
                    dve.tensor_scalar(norm[:, t, :], resid[:, t, :], negm[:, 0, t:t + 1], rstd[:, 0, t:t + 1],
                                      ALU.add, ALU.mult).then_inc(s_n1, 1)

            dve.wait_ge(s_bias, 16)
            step(dve.tensor_scalar(b_over_d[:, :, :], b_nat[:, :, :], 1.0 / D, None, ALU.mult))
            dve.wait_ge(s_const, 3)

            def row_addition(c, hs):
                step(dve.tensor_reduce(row_add[:, c, hs], w_nat[:, hs, c, :], AX, ALU.add))
                step(dve.scalar_tensor_tensor(row_add[:, c, hs], row_add[:, c, hs], -1.0 / D, b_over_d[:, hs, c],
                                              ALU.mult, ALU.add))

            for i in range(4):
                dve.wait_ge(s_w[i], 16)
                hs = slice(2 * i, 2 * i + 2)
                row_addition(1, hs)
                dve.wait_ge(s_q_sum, 2 * i + 2)
                dve.scalar_tensor_tensor(row_add[:, 0, hs], row_add[:, 0, hs], -1.0 / D, b_over_d[:, hs, 0],
                                         ALU.mult, ALU.add).then_inc(s_q_add, 1)
                for hp in range(2):
                    r = slice(64 * hp, 64 * hp + 64)
                    dve.tensor_tensor(wk_blk[r, hs, D * hp:D * hp + D], w_nat[r, hs, 1, :],
                                      row_add[r, 1, hs].unsqueeze(2).to_broadcast([64, 2, D]), ALU.add
                                      ).then_inc(s_wprep, 1)
                if i == 1:
                    first_norm()
            def value_weights():
                row_addition(2, slice(0, HP))
                dve.tensor_tensor(wv_c, w_nat[:, :, 2, :], row_add[:, 2, :].unsqueeze(2).to_broadcast([P, HP, D]),
                                  ALU.add).then_inc(s_wprep, 1)

            def low(dst, src, const, high, s_done):
                dve.scalar_tensor_tensor(dst, src, const, high.bitcast(F32), ALU.add, ALU.subtract).then_inc(s_done, 1)

            def g_low(i, n):
                dve.wait_ge(s_set_ev, n)
                low(G[1][:, 4 * i:4 * i + 4, :], ps[:, G_BANK[i], :].rearrange("p (h n) -> p h n", n=D), 0.0,
                    G[0][:, 4 * i:4 * i + 4, :], s_set_lo)

            def n_low(i):
                dve.wait_ge(s_set_ev, 3 + i)
                cols = slice(512 * i, 512 * i + 512)
                low(n_parts[:, 1, cols], ps[:, 6 + i, :], 1.0, n_parts[:, 0, cols], s_set_lo)

            def prepare_low(n):
                dve.wait_ge(s_set_ev, N1T_OUT + n + 3)
                low(wvT[:, 1, 512 * n:512 * n + 512], ps[:, 6 + n, :], 0.0, wvT[:, 0, 512 * n:512 * n + 512], s_set_lo)

            def t_low(b, u):
                k = HP * b + u
                dve.wait_ge(s_t_hi, k + 1)
                bank = ps[:, ring_bank[("T", b, u)], :]
                heads = slice(2 * (k % 6), 2 * (k % 6) + 2)
                dve.tensor_tensor(t_ring[1][:, heads, :], bank.rearrange("p (h q) -> p h q", h=2),
                                  t_ring[0][:, heads, :].bitcast(F32), ALU.subtract).then_inc(s_t_lo, 1)

            n_low(0)
            g_low(0, 1)
            g_low(1, 2)
            t_low(0, 0)
            t_low(0, 1)
            g_low(2, 5)
            g_low(3, 6)
            n_low(1)

            def cross_values(i):
                dve.wait_ge(s_vx, i + 1)
                dve.wait_ge(s_wx, 144)
                dve.wait_ge(s_const, 6)
                dve.tensor_tensor(v_heads[:, 4 * i:4 * i + 4, :, 0:DH],
                                  ps[:, 6 + i, :].rearrange("p (t h d) -> p t h d", t=4, h=H),
                                  brow[:, 1, :].rearrange("p (h d) -> p h d", d=DH).unsqueeze(1).to_broadcast([P, 4, H, DH]),
                                  ALU.add).then_inc(s_vx_ev, 1)

            def maxima(b, u):
                k = 12 * b + u
                dve.wait_ge(s_sc, k + 1)
                j = u // 3
                if u % 3 < 2:
                    dst, n = negmax[:, 0, 4 * j + 2 * (u % 3):4 * j + 2 * (u % 3) + 2], 2
                else:
                    dst, n = negmax[:, 1, 4 * j:4 * j + 4], 4
                dve.tensor_reduce(dst, ps[:, k % 3, :].rearrange("p (h q) -> p h q", h=n), AX, ALU.max,
                                  negate=True).then_inc(s_max, 1)

            def values_out(b, u):
                kt, hf = u % 2, u // 2
                dve.wait_ge(s_exp, 12 * b + 6 * hf + 6)
                hs = slice(8 * hf, 8 * hf + 8)
                step(dve.reciprocal(rsum[:, kt, hs], psums[:, kt, hs]))
                dve.wait_ge(s_v, 4 * b + u + 1)
                if b >= 1:
                    dve.wait_ge(s_z, 4 * (b - 1) + 2 * hf + 2)
                dve.tensor_tensor(v_sb[:, kt, 512 * hf:512 * hf + 512].rearrange("p (h e) -> p h e", e=E1),
                                  ps[:, ring_bank[("V", b, u)], :].rearrange("p (h e) -> p h e", e=E1),
                                  rsum[:, kt, hs].unsqueeze(2).to_broadcast([P, 8, E1]), ALU.mult).then_inc(s_v_ev, 1)

            def residual(n, b, s_done, count, s_stat):
                ts = slice(TPB * b, TPB * b + TPB)
                dve.tensor_tensor(resid[:, ts, :], ps[:, 7, 0:S].rearrange("p (t d) -> p t d", d=D),
                                  resid[:, ts, :], ALU.add).then_inc(s_done, 1)
                dve.wait_ge(s_done, count)
                for t in range(TPB * b, TPB * b + TPB):
                    step(dve.bn_stats(stats[:, t, :], resid[:, t, :]))
                    dve.bn_aggr(mv[:, n, t, :], stats[:, t, :]).then_inc(s_stat, 1)

            def cross_max(b, u):
                g, qt = u // 2, u % 2
                dve.wait_ge(s_mx, 16 * b + u + 1)
                if u == 0 and b >= 1:
                    dve.wait_ge(s_misc, misc_at[("mT", b - 1)] + 1)
                dve.tensor_reduce(mneg[:, qt, :].rearrange("p (r g) -> p r g", r=2)[:, :, g],
                                  ps[:, max_bank[("MX", b, u)], :].rearrange("p (h k) -> p h k", h=2), AX, ALU.max,
                                  negate=True).then_inc(s_mx_ev, 1)

            def self_residual(b):
                dve.wait_ge(s_misc, misc_at[("PJ", b)] + 1)
                dve.wait_ge(s_xb, 1)
                residual(1, b, s_misc_ev, misc_at[("PJ", b)] + 1, s_mv2)

            def cross_normalise(b, qt):
                dve.wait_ge(s_misc, misc_at[(f"oq{qt}", b)] + 1)
                turned = ps[:, 7, :].rearrange("p (g j r) -> p g j r", g=4, j=4)
                step(dve.reciprocal(r_den[:, qt, :].rearrange("p (g j) -> p g j", g=4), turned[:, :, :, DH]))
                for par in range(2):
                    src = turned[:, :, :, :].rearrange("p g (a r) c -> p g a r c", r=2)[:, :, :, par, 0:DH]
                    den = r_den[:, qt, :].rearrange("p (g a r) -> p g a r", g=4, r=2)[:, :, :, par]
                    last = (dve.tensor_tensor(o_n[:, qt, 64 * par:64 * par + 64].rearrange("p (g a d) -> p g a d", g=4, d=DH),
                                           src, den.unsqueeze(3).to_broadcast([P, 4, 2, DH]), ALU.mult))
                last.then_inc(s_misc_ev, 1)

            def cross_residual(b):
                dve.wait_ge(s_misc, misc_at[("wo", b)] + 1)
                dve.wait_ge(s_xb2, b + 1)
                residual(2, b, s_misc_ev, misc_at[("wo", b)] + 1, s_mv3)

            def weight_low(i):
                dve.wait_ge(s_whi, i + 1)
                cols = slice(512 * i, 512 * i + 512)
                dve.tensor_tensor(w1_lo[:, cols], w1_raw[:, cols], w1_hi[:, cols].bitcast(F32), ALU.subtract
                                  ).then_inc(s_wlo, 1)

            def norm_low(hf):
                dve.wait_ge(s_n3T, hf + 1)
                cols = slice(512 * hf, 512 * hf + 512)
                low(n_parts[:, 1, cols], ps[:, 7, :], 0.0, n_parts[:, 0, cols], s_misc_ev)

            def best_two(hf):
                ts = slice(4 * hf, 4 * hf + 4)
                dve.wait_ge(s_misc, misc_at[("RT", hf)] + 1)
                step(dve.tensor_copy(score[:, ts, :], ps[:, 7, 0:4 * NE].rearrange("p (t e) -> p t e", e=NE)))
                dve.tensor_tensor(score[:, ts, :], score[:, ts, :], br_row[:, :].unsqueeze(1).to_broadcast([P, 4, NE]),
                                  ALU.add).then_inc(s_misc_ev, 1)
                dve.wait_ge(s_misc_ev, misc_at[("RT", hf)] + 1)
                for t in range(4 * hf, 4 * hf + 4):
                    step(dve.max(top[:, t, :], score[:, t, :]))
                    last = dve.max_index(top_i[:, t, :], top[:, t, :], score[:, t, :])
                last.then_inc(s_score, 1)
                dve.wait_ge(s_score, 2 * hf + 1)
                dve.tensor_tensor(gate[:, 0, ts], top[:, ts, 1], top[:, ts, 0], ALU.subtract).then_inc(s_score, 1)

            def gates(hf):
                ts = slice(4 * hf, 4 * hf + 4)
                step(dve.tensor_copy(top_f[:, ts, :], top_i[:, ts, 0:2]))
                for n in range(2):
                    step(dve.tensor_tensor(hot[:, n, ts, :], iota8[:, :].unsqueeze(1).to_broadcast([P, 4, NE]),
                                           top_f[:, ts, n:n + 1].to_broadcast([P, 4, NE]), ALU.is_equal))
                dve.wait_ge(s_ed, hf + 1)
                step(dve.tensor_scalar(gate[:, 2, ts], gate[:, 1, ts], 1.0, None, ALU.add))
                step(dve.reciprocal(gate[:, 2, ts], gate[:, 2, ts]))
                step(dve.tensor_tensor(gate[:, 3, ts], gate[:, 1, ts], gate[:, 2, ts], ALU.mult))
                for n in range(2):
                    step(dve.tensor_tensor(hot[:, n, ts, :], hot[:, n, ts, :],
                                           gate[:, 2 + n, ts].unsqueeze(2).to_broadcast([P, 4, NE]), ALU.mult))
                dve.tensor_tensor(wgt[:, ts, :], hot[:, 0, ts, :], hot[:, 1, ts, :], ALU.add).then_inc(s_wgt, 1)
                dve.wait_ge(s_wgt, hf + 1)

            def relu(k, c):
                dve.wait_ge(s_h, 4 * k + c + 1)
                ge(dve, s_y, k - 1)
                dve.tensor_scalar(hid[:, k % 2, c, :], ps[:, H_BANK[c], :], b1T[:, NC * (k % NE) + c:NC * (k % NE) + c + 1],
                                  0.0, ALU.add, ALU.max).then_inc(s_hd, 1)

            def bias_sum(hf):
                ts = slice(4 * hf, 4 * hf + 4)
                dve.wait_ge(s_misc, misc_at[("B2", hf)] + 1)
                dve.wait_ge(s_n3, 4 * hf + 4)
                ge(dve, s_acc, accumulated(hf))
                dve.tensor_tensor(resid[:, ts, :], ps[:, 7, :].rearrange("p (t d) -> p t d", d=D),
                                  resid[:, ts, :], ALU.add).then_inc(s_misc_ev, 1)
                dve.wait_ge(s_misc_ev, misc_at[("B2", hf)] + 1)

            def accumulate(k):
                e, hf = k % NE, k // NE
                dve.wait_ge(s_y, k + 1)
                dve.wait_ge(s_n3, 4 * hf + 4)
                ge(dve, s_acc, k)
                for tt in range(4):
                    t = 4 * hf + tt
                    last = dve.scalar_tensor_tensor(resid[:, t, :], ps[:, Y_BANK[k % 2], P * tt:P * tt + P],
                                                    wgt[:, t, e:e + 1], resid[:, t, :], ALU.mult, ALU.add)
                last.then_inc(s_acc, 1)

            pending = []
            for slot in slots[2:]:
                fresh = [k for k in slot if k[0] == "T" or k in (("P", 0, 2), ("P", 0, 3))]
                if slot[0][0] == "S":
                    maxima(*slot[0][1:])
                    pending, fresh = fresh, pending
                else:
                    fresh, pending = pending + fresh, []
                for kind, b, u in fresh:
                    if kind == "T":
                        t_low(b, u)
                    else:
                        prepare_low(u - 2)
                for kind, b, *i in slot:
                    if kind == "V":
                        values_out(b, *i)
                    elif kind == "P" and i[0] == 0:
                        value_weights()
                    elif kind == "P" and i[0] >= 8:
                        cross_values(i[0] - 8)
                    elif kind == "PJ":
                        self_residual(b)
                    elif kind == "MX":
                        cross_max(b, *i)
                    elif kind == "q" and b == B - 1:
                        split_q(dve, step, b)
                    elif kind == "mT" and b >= 1:
                        split_m(dve, step, b)
                    elif kind in ("oq0", "oq1"):
                        cross_normalise(b, int(kind == "oq1"))
                    elif kind == "wo":
                        cross_residual(b)
                    elif kind == "WS":
                        weight_low(*i)
                    elif kind == "NT":
                        norm_low(b)
                    elif kind == "RT":
                        best_two(b)
                    elif kind == "GT":
                        gates(b)
                    elif kind == "B2":
                        bias_sum(b)
                    elif kind == "H" and i[0] % 2 == 1:
                        relu(b, *i)
                    elif kind == "Y":
                        accumulate(b)


_INS = ['x', 'ctx_1024', 'L0_attn_W_qkv', 'L0_attn_b_qkv', 'L0_attn_W_o', 'L0_attn_b_o',
        'L0_xattn_Wq', 'L0_xattn_bq', 'L0_xattn_Wk', 'L0_xattn_bk', 'L0_xattn_Wv', 'L0_xattn_bv',
        'L0_xattn_Wo', 'L0_xattn_bo', 'L0_ffn_Wr', 'L0_ffn_br', 'L0_ffn_W1', 'L0_ffn_b1', 'L0_ffn_W2', 'L0_ffn_b2']


def kernel(**inputs):
    import numpy as _np
    import concourse.bacc as _bacc
    from concourse import mybir as _mybir
    from concourse.bass_utils import run_bass_kernel_spmd as _run

    nc = _bacc.Bacc("TRN2", target_bir_lowering=False, num_devices=1)
    arrays, args = {}, []
    for name in _INS:
        a = _np.ascontiguousarray(inputs[name])
        arrays[f"in_{name}"] = a
        args.append(nc.dram_tensor(f"in_{name}", a.shape, _mybir.dt.from_np(a.dtype), kind="ExternalInput").ap())
    shape = arrays["in_x"].shape
    args.append(nc.dram_tensor("out_dram", shape, _mybir.dt.float32, kind="ExternalOutput").ap())
    decoder_layer(nc, *args)
    r = _run(nc, [arrays], core_ids=[0])
    return r.results[0]["out_dram"]
```
